# Optimizing a Trainium2 kernel written in Bass

```python
import numpy as np
import jax
import jax.numpy as jnp

def _softmax(x, axis=-1):
    return jax.nn.softmax(x, axis=axis)

def _gelu(x):
    return jax.nn.gelu(x, approximate=True)

def _silu(x):
    return jax.nn.silu(x)

def _sigmoid(x):
    return jax.nn.sigmoid(x)

def _layernorm(x, axis=-1, eps=1e-05):
    m = jnp.mean(x, axis=axis, keepdims=True)
    v = jnp.var(x, axis=axis, keepdims=True)
    return (x - m) / jnp.sqrt(v + eps)

def _scatter_add(tgt, idx, src, axis=0):
    return tgt.at[idx].add(src)

def _segment_sum(src, seg, n):
    return jax.ops.segment_sum(src, seg, n)
kernel_name = 'mk_decoder_preln_d1_seqx_r2_cdab16'

def setup_inputs(seed: int=0):
    np.random.seed(seed)
    _w = jnp.asarray

    def _rec_inputs():
        import jax
        import jax.numpy as jnp
        _rk = jax.random.key(seed)
        x = 0.0001212 + 1 * jax.random.normal(jax.random.fold_in(_rk, 1), (4, 1024, 1024), jnp.float32)
        _lenS = 1024 - jax.random.randint(jax.random.fold_in(_rk, 7), (4,), 0, max(1, 1024 // 4) + 1, jnp.int32)
        _lenS2 = 1024 - jax.random.randint(jax.random.fold_in(_rk, 8), (4,), 0, max(1, 1024 // 4) + 1, jnp.int32)
        _ctx_2048P = jax.random.normal(jax.random.fold_in(_rk, 11), (4, 16, 1024), jnp.float32)
        _ctx_2048c = jax.random.dirichlet(jax.random.fold_in(_rk, 511), 0.3 * jnp.ones((16,), jnp.float32), (4, 1024))
        _ctx_2048t = jnp.einsum('bsk,bkd->bsd', _ctx_2048c, _ctx_2048P)
        _ctx_2048t = _ctx_2048t * jax.lax.rsqrt(jnp.mean(jnp.square(_ctx_2048t)) + 1e-12) * 0.953939
        ctx_2048 = 0.000173663 + 1.0001 * (_ctx_2048t + 0.3 * jax.random.normal(jax.random.fold_in(_rk, 611), (4, 1024, 1024), jnp.float32))
        return (x, ctx_2048)
    x, ctx_2048 = _rec_inputs()

    def _L0_attn_setup():
        import jax, jax.numpy as jnp
        import numpy as np
        EPS = 1e-15
        HEAD_DIM = 32
        PAD_VAL = 1.0
        key = jax.random.key(seed)
        k1, k2, k3, k4 = jax.random.split(key, 4)
        B, N, C = (2, 2048, 1024)
        s = 1.0 / np.sqrt(C).astype(np.float32)
        x = jax.random.normal(k1, (B, N, C), jnp.float32)
        w_qkv = jax.random.normal(k2, (3 * C, C), jnp.float32) * s
        w_proj = jax.random.normal(k3, (C, C), jnp.float32) * s
        b_proj = jax.random.normal(k4, (C,), jnp.float32) * 0.01
        return {'x': x, 'w_qkv': w_qkv, 'w_proj': w_proj, 'b_proj': b_proj}
    _L0_attn_all = _L0_attn_setup()
    _L0_attn_in = {k: v for k, v in _L0_attn_all.items() if k in ('w_qkv', 'w_proj', 'b_proj')}
    del _L0_attn_all

    def _L0_xattn_setup():
        import jax, jax.numpy as jnp
        import numpy as np
        B_DIM, T_DIM, C_DIM = (16, 512, 1024)

        def _wkv(w, u, k, v):
            Bn, Tn, Cn = k.shape
            NEG_INF = jnp.float32(-1e+38)

            def step(carry, kv_t):
                p, q, o = carry
                kt, vt = kv_t
                no = jnp.maximum(o, u + kt)
                A = jnp.exp(o - no)
                E = jnp.exp(u + kt - no)
                y = (A * p + E * vt) / (A * q + E)
                no2 = jnp.maximum(w + o, kt)
                A2 = jnp.exp(w + o - no2)
                E2 = jnp.exp(kt - no2)
                return ((A2 * p + E2 * vt, A2 * q + E2, no2), y)
            init = (jnp.zeros((Bn, Cn), k.dtype), jnp.zeros((Bn, Cn), k.dtype), jnp.full((Bn, Cn), NEG_INF, k.dtype))
            kT = jnp.moveaxis(k, 1, 0)
            vT = jnp.moveaxis(v, 1, 0)
            _, yT = jax.lax.scan(step, init, (kT, vT))
            return jnp.moveaxis(yT, 0, 1)
        key = jax.random.key(seed)
        k1, k2, k3, k4 = jax.random.split(key, 4)
        w = -jnp.exp(jax.random.normal(k1, (C_DIM,), jnp.float32))
        u = jax.random.normal(k2, (C_DIM,), jnp.float32)
        k = jax.random.normal(k3, (B_DIM, T_DIM, C_DIM), jnp.float32)
        v = jax.random.normal(k4, (B_DIM, T_DIM, C_DIM), jnp.float32)
        return {'B': B_DIM, 'T': T_DIM, 'C': C_DIM, 'w': w, 'u': u, 'k': k, 'v': v}
    _L0_xattn_all = _L0_xattn_setup()
    _L0_xattn_in = {k: v for k, v in _L0_xattn_all.items() if k in ('w', 'u')}
    del _L0_xattn_all

    def _L0_ffn_setup():
        import jax, jax.numpy as jnp
        import numpy as np
        B, L, D = (4, 2048, 1024)
        DF = 4 * D
        CAPACITY_RATIO = 0.5
        key = jax.random.key(seed)
        ks = jax.random.split(key, 4)
        s = 0.02
        return {'x': jax.random.normal(ks[0], (B, L, D), dtype=jnp.float32), 'w_r': jax.random.normal(ks[1], (D,), dtype=jnp.float32) * s, 'b_r': jnp.zeros((), dtype=jnp.float32), 'w1': jax.random.normal(ks[2], (D, DF), dtype=jnp.float32) * s, 'b1': jnp.zeros((DF,), dtype=jnp.float32), 'w2': jax.random.normal(ks[3], (DF, D), dtype=jnp.float32) * s, 'b2': jnp.zeros((D,), dtype=jnp.float32)}
    _L0_ffn_all = _L0_ffn_setup()
    _L0_ffn_in = {k: v for k, v in _L0_ffn_all.items() if k in ('w_r', 'b_r', 'w1', 'b1', 'w2', 'b2')}
    del _L0_ffn_all
    return {'x': x, 'ctx_2048': ctx_2048, 'L0_attn_w_qkv': _L0_attn_in['w_qkv'], 'L0_attn_w_proj': _L0_attn_in['w_proj'], 'L0_attn_b_proj': _L0_attn_in['b_proj'], 'L0_xattn_w': _L0_xattn_in['w'], 'L0_xattn_u': _L0_xattn_in['u'], 'L0_ffn_w_r': _L0_ffn_in['w_r'], 'L0_ffn_b_r': _L0_ffn_in['b_r'], 'L0_ffn_w1': _L0_ffn_in['w1'], 'L0_ffn_b1': _L0_ffn_in['b1'], 'L0_ffn_w2': _L0_ffn_in['w2'], 'L0_ffn_b2': _L0_ffn_in['b2']}

def reference(x, ctx_2048, L0_attn_w_qkv, L0_attn_w_proj, L0_attn_b_proj, L0_xattn_w, L0_xattn_u, L0_ffn_w_r, L0_ffn_b_r, L0_ffn_w1, L0_ffn_b1, L0_ffn_w2, L0_ffn_b2):
    import jax
    import jax.numpy as jnp

    def _L0_attn_ref(x, w_qkv, w_proj, b_proj):
        import jax, jax.numpy as jnp
        import numpy as np
        EPS = 1e-15
        HEAD_DIM = 32
        PAD_VAL = 1.0
        B, N, C = x.shape
        d = HEAD_DIM
        h = C // d
        qkv = (x @ w_qkv.T).reshape(B, N, 3, C)
        q, k, v = (qkv[:, :, 0], qkv[:, :, 1], qkv[:, :, 2])

        def to_heads(t):
            return t.reshape(B, N, h, d).transpose(0, 2, 3, 1)
        q = jax.nn.relu(to_heads(q))
        k = jax.nn.relu(to_heads(k))
        v = to_heads(v)
        v_pad = jnp.pad(v, ((0, 0), (0, 0), (0, 1), (0, 0)), constant_values=PAD_VAL)
        vk = jnp.einsum('bhen,bhdn->bhed', v_pad, k)
        out = jnp.einsum('bhed,bhdn->bhen', vk, q)
        out = out[:, :, :-1] / (out[:, :, -1:] + EPS)
        out = out.reshape(B, C, N).transpose(0, 2, 1)
        return out @ w_proj.T + b_proj

    def _L0_xattn_ref(B, T, C, w, u, k, v):
        import jax, jax.numpy as jnp
        import numpy as np
        B_DIM, T_DIM, C_DIM = (16, 512, 1024)

        def _wkv(w, u, k, v):
            Bn, Tn, Cn = k.shape
            NEG_INF = jnp.float32(-1e+38)

            def step(carry, kv_t):
                p, q, o = carry
                kt, vt = kv_t
                no = jnp.maximum(o, u + kt)
                A = jnp.exp(o - no)
                E = jnp.exp(u + kt - no)
                y = (A * p + E * vt) / (A * q + E)
                no2 = jnp.maximum(w + o, kt)
                A2 = jnp.exp(w + o - no2)
                E2 = jnp.exp(kt - no2)
                return ((A2 * p + E2 * vt, A2 * q + E2, no2), y)
            init = (jnp.zeros((Bn, Cn), k.dtype), jnp.zeros((Bn, Cn), k.dtype), jnp.full((Bn, Cn), NEG_INF, k.dtype))
            kT = jnp.moveaxis(k, 1, 0)
            vT = jnp.moveaxis(v, 1, 0)
            _, yT = jax.lax.scan(step, init, (kT, vT))
            return jnp.moveaxis(yT, 0, 1)
        return _wkv(w, u, k, v)

    def _L0_ffn_ref(x, w_r, b_r, w1, b1, w2, b2):
        import jax, jax.numpy as jnp
        import numpy as np
        B, L, D = (4, 2048, 1024)
        DF = 4 * D
        CAPACITY_RATIO = 0.5
        b, l, d = x.shape
        k = int(l * CAPACITY_RATIO)
        scores = jnp.einsum('bld,d->bl', x, w_r) + b_r
        _, idx = jax.lax.top_k(scores, k)
        x_sel = jnp.take_along_axis(x, idx[:, :, None], axis=1)
        h = jax.nn.gelu(jnp.einsum('bkd,df->bkf', x_sel, w1) + b1)
        out_sel = jnp.einsum('bkf,fd->bkd', h, w2) + b2
        batch_ix = jnp.arange(b)[:, None]
        out = jnp.zeros_like(x).at[batch_ix, idx].set(out_sel)
        return out
    x = x + _L0_attn_ref(_layernorm(x, axis=-1), L0_attn_w_qkv, L0_attn_w_proj, L0_attn_b_proj)
    x = x + _L0_xattn_ref(4, 1024, 1024, L0_xattn_w, L0_xattn_u, _layernorm(x, axis=-1), ctx_2048)
    x = x + _L0_ffn_ref(_layernorm(x, axis=-1), L0_ffn_w_r, L0_ffn_b_r, L0_ffn_w1, L0_ffn_b1, L0_ffn_w2, L0_ffn_b2)
    return x

_drawn_inputs = setup_inputs


def setup_inputs(seed=0):
    import zlib

    import numpy as np

    out = dict(_drawn_inputs(seed))
    spreads = {'L0_ffn_b1': (0.0, 0.1), 'L0_ffn_b2': (0.0, 0.1)}
    factors = {'L0_attn_b_proj': 7.55}
    for name, (base, spread) in spreads.items():
        noise = np.random.default_rng([zlib.crc32(name.encode()), seed]).standard_normal(out[name].shape)
        drawn = base * np.exp(spread * noise) if base else spread * noise
        out[name] = jnp.asarray(drawn.astype(out[name].dtype))
    for name, factor in factors.items():
        out[name] = (out[name] * factor).astype(out[name].dtype)
    return out
```

```python
from contextlib import ExitStack

import concourse.bass as bass
from concourse import mybir

F32 = mybir.dt.float32
F32R = mybir.dt.float32r
I32 = mybir.dt.int32
ACT = mybir.ActivationFunctionType
ALU = mybir.AluOpType
ds = bass.ds

P = 128
B, T, C = 4, 1024, 1024
KT = C // P
TT = T // P
HALF = 512
HEAD = 32
DF = 4 * C
SEL = T // 2
CHUNK = 512
STEPS = DF // CHUNK
LN_EPS = 1e-5
ATT_EPS = 1e-15
NO_PAST = -1e38
R_CLAMP = 60.0


class Tools:

    def __init__(self, nc, ctx, tag):
        self.nc, self.ctx, self.tag = nc, ctx, tag

    def sb(self, name, shape, dt=F32):
        return self.ctx.enter_context(self.nc.sbuf_tensor(f"{self.tag}_{name}", shape, dt))

    def ps(self, name, shape):
        return self.ctx.enter_context(self.nc.psum_tensor(f"{self.tag}_{name}", shape, F32))

    def sem(self, name):
        return self.ctx.enter_context(self.nc.semaphore(f"{self.tag}_{name}"))


def hold(engine, sem, value, spare):
    engine.wait_ge(sem, value)
    engine.sem_inc(spare, 1)


def product3(pe, out, w_hi, w_lo, x_hi, x_lo, start, stop):
    pe.matmul(out, w_hi, x_hi, start=start, stop=False)
    pe.matmul(out, w_hi, x_lo, start=False, stop=False)
    return pe.matmul(out, w_lo, x_hi, start=False, stop=stop)


def attention_phase(nc, x, w_kvq, w_p, b_p, consts_mask, ident_in, x1_dram, kT_dram):
    with ExitStack() as ctx:
        m = Tools(nc, ctx, "att")
        x_tok = m.sb("x_tok", [P, 2, C])
        xn = m.sb("xn", [P, 2, C])
        act_hi = m.sb("act_hi", [P, KT, T], F32R)
        act_lo = m.sb("act_lo", [P, KT, T], F32R)
        w_raw = m.sb("w_raw", [P, 2, 2048])
        w_hi = m.sb("w_hi", [P, 2, 2048], F32R)
        w_lo = m.sb("w_lo", [P, 2, 2048], F32R)
        kvb_hi = m.sb("kvb_hi", [P, KT, 256], F32R)
        kvb_lo = m.sb("kvb_lo", [P, KT, 256], F32R)
        kvb = m.sb("kvb", [P, 256])
        kT = m.sb("kT", [P, 2, KT, P])
        bias = m.sb("bias", [P, C])
        mask = m.sb("mask", [P, P])
        ident = m.sb("ident", [P, P])
        stats = m.sb("stats", [P, 2, 6])
        mv = m.sb("mv", [P, 2])
        var_eps = m.sb("var_eps", [P, 1])
        minus_half = m.sb("minus_half", [P, 1])
        rstd = m.sb("rstd", [P, 1])
        with ExitStack() as kv_only:
            k = Tools(nc, kv_only, "attk")
            kv_hi = k.sb("kv_hi", [P, TT, 258], F32R)
            kv_lo = k.sb("kv_lo", [P, TT, 258], F32R)
        q_hi = m.sb("q_hi", [P, 2, HALF], F32R)
        q_lo = m.sb("q_lo", [P, 2, HALF], F32R)
        rden = m.sb("rden", [P, HALF])
        o = m.sb("o", [P, KT, T])
        pair = [m.ps(f"pair{i}", [P, 2, HALF]) for i in range(4)]

        const_in = m.sem("const_in")
        x_loaded = [m.sem(f"x_loaded{s}") for s in range(2)]
        stat_step, var_ready, rstd_ready = m.sem("stat_step"), m.sem("var_ready"), m.sem("rstd_ready")
        half_set = m.sem("half_set")
        xn_ready, tr_done = m.sem("xn_ready"), m.sem("tr_done")
        xt_hi, xt_lo = m.sem("xt_hi"), m.sem("xt_lo")
        raw_loaded = [m.sem(f"raw_loaded{s}") for s in range(2)]
        w_hi_ready, w_lo_ready = m.sem("w_hi_ready"), m.sem("w_lo_ready")
        kv_main, kv_hi_ready, kv_lo_ready = m.sem("kv_main"), m.sem("kv_hi_ready"), m.sem("kv_lo_ready")
        kv_free, vk_done = m.sem("kv_free"), m.sem("vk_done")
        ones_set = m.sem("ones_set")
        kvb_hi_ready, kvb_lo_ready = m.sem("kvb_hi_ready"), m.sem("kvb_lo_ready")
        kvb_made = m.sem("kvb_made")
        q_main, q_hi_ready, q_lo_ready = m.sem("q_main"), m.sem("q_hi_ready"), m.sem("q_lo_ready")
        nd_done, o_done, rden_step = m.sem("nd_done"), m.sem("o_done"), m.sem("rden_step")
        wp_lo_dve = m.sem("wp_lo_dve")
        os_hi_ready, os_lo_ready = m.sem("os_hi_ready"), m.sem("os_lo_ready")
        xb_ready, proj_done, x1_ready = m.sem("xb_ready"), m.sem("proj_done"), m.sem("x1_ready")
        x1_stored = [m.sem(f"x1_stored{s}") for s in range(2)]
        kt_evac = m.sem("kt_evac")
        kt_stored = [m.sem(f"kt_stored{s}") for s in range(2)]
        held = {e: m.sem(f"held_{e}") for e in ("sp", "act", "pool", "pe", "dve")}
        block = ctx.enter_context(nc.Block())

        def w_view(w, s):
            return w[:, s, :].rearrange("p (k n) -> p k n", k=KT)

        def o_view(w, s):
            return w[:, s, 0:KT * P].rearrange("p (k n) -> p k n", k=KT)

        @block.sync
        def _(sp):
            sp.dma_start(mask[:], consts_mask).then_inc(const_in, 16)
            sp.dma_start(ident[:], ident_in).then_inc(const_in, 16)
            sp.dma_start(bias[:], b_p.rearrange("(a n) -> a n", a=1).to_broadcast([P, C])).then_inc(const_in, 16)

            def load_weights(b, idx, s, src, row):
                sp.wait_ge(w_lo_ready, b * 16 + idx + 1)
                sp.dma_start(w_raw[:, s, :], src[ds(row * P, P), :]).then_inc(raw_loaded[s], 16)

            def load_x(b, n, t, s):
                sp.wait_ge(xn_ready, b * 16 + n + 1)
                sp.dma_start(x_tok[:, s, :], x[ds(b * T + t * P, P), :]).then_inc(x_loaded[s], 16)

            def store_x1(b, t, s):
                sp.wait_ge(x1_ready, b * 8 + t + 1 + 2)
                sp.dma_start(x1_dram[ds(b * T + t * P, P), :], x_tok[:, s, :]).then_inc(x1_stored[s], 16)

            with sp.Fori(0, B) as b:
                for s in range(2):
                    load_x(b, s, s, s)
                    load_weights(b, s, s, w_kvq, s)
                with sp.Fori(1, TT // 2) as i:
                    for s in range(2):
                        load_x(b, i * 2 + s, i * 2 + s, s)
                for s in range(2):
                    load_x(b, 8 + s, s, s)
                with sp.Fori(1, 6) as i:
                    for s in range(2):
                        load_weights(b, i * 2 + s, s, w_kvq, i * 2 + s)
                with sp.Fori(0, 2) as i:
                    for s in range(2):
                        load_weights(b, i * 2 + s + 12, s, w_p, i * 2 + s)
                with sp.Fori(0, TT // 2 - 1) as i:
                    for s in range(2):
                        store_x1(b, i * 2 + s, s)
                        hold(sp, x1_stored[s], b * 64 + i * 16 + 16, held["sp"])
                        load_x(b, i * 2 + s + 10, i * 2 + s + 2, s)
                for s in range(2):
                    store_x1(b, TT - 2 + s, s)
                for s in range(2):
                    hold(sp, x1_stored[s], b * 64 + 64, held["sp"])

        def layer_norm(dve, src, dst, n):
            for h in range(2):
                dve.bn_stats(stats[:, h, :], src[:, h * HALF:(h + 1) * HALF]).then_inc(stat_step, 1)
            dve.wait_ge(xn_ready, n + 2)
            hold(dve, stat_step, n * 3 + 2, held["dve"])
            dve.bn_aggr(mv[:], stats[:]).then_inc(stat_step, 1)
            dve.wait_ge(stat_step, n * 3 + 3)
            dve.tensor_scalar(var_eps[:], mv[:, 1:2], LN_EPS, None, ALU.add).then_inc(var_ready, 1)
            dve.wait_ge(rstd_ready, n + 1)
            return dve.tensor_scalar(dst, src, mv[:, 0:1], rstd[:, 0:1], ALU.subtract, ALU.mult)

        @block.vector
        def _(dve):
            dve.sem_inc(xn_ready, 2)
            dve.sem_inc(xt_lo, 2)
            dve.sem_inc(kv_lo_ready, 4)
            dve.sem_inc(kvb_made, 4)
            dve.sem_inc(q_lo_ready, 4)
            dve.sem_inc(o_done, 2)
            dve.sem_inc(x1_ready, 2)
            dve.sem_inc(kvb_lo_ready, 1)
            dve.wait_ge(const_in, 48)
            with dve.Fori(0, B) as b:
                def norm(t):
                    s = t % 2
                    dve.wait_ge(x_loaded[s], b * 128 + t // 2 * 16 + 16)
                    dve.wait_ge(tr_done, b * 16 + t + 1)
                    layer_norm(dve, x_tok[:, s, :], xn[:, s, :], b * 16 + t).then_inc(xn_ready, 1)

                def low_xt(t):
                    dve.wait_ge(xt_hi, b * 8 + t + 1)
                    dve.tensor_tensor(act_lo[:, :, t * P:(t + 1) * P], pair[3][:].rearrange("p a (k t) -> p (a k) t", t=P),
                                      act_hi[:, :, t * P:(t + 1) * P].bitcast(F32), ALU.subtract).then_inc(xt_lo, 1)

                def low_kv(g, t):
                    bank = pair[t % 4 // 2][:, t % 2, :]
                    dve.wait_ge(kv_hi_ready, (b * 8 + g) * 8 + t + 1)
                    dve.scalar_tensor_tensor(kv_lo[:, t, 0:P], bank[:, 0:P], 0.0, kv_hi[:, t, 0:P].bitcast(F32),
                                             ALU.max, ALU.subtract)
                    dve.tensor_tensor(kv_lo[:, t, P:2 * P], bank[:, P:2 * P], kv_hi[:, t, P:2 * P].bitcast(F32),
                                      ALU.subtract).then_inc(kv_lo_ready, 1)

                def head_blocks(g, s):
                    vk = pair[2][:, s, :]
                    dve.wait_ge(kvb_lo_ready, b * 8 + g + 1)
                    dve.wait_ge(vk_done, b * 8 + g + 1 + 1)
                    dve.tensor_tensor(kvb[:, 0:P], vk[:, 0:P], mask[:], ALU.mult).then_inc(kvb_made, 1)
                    dve.tensor_scalar(kvb[:, P:2 * P], mask[:], vk[:, P:P + 1], None, ALU.mult).then_inc(kvb_made, 1)
                    dve.wait_ge(kvb_hi_ready, b * 8 + g + 1)
                    dve.tensor_tensor(kvb_lo[:, ds(g, 1), :].rearrange("p a n -> p (a n)"),
                                      kvb[:], kvb_hi[:, ds(g, 1), :].rearrange("p a n -> p (a n)").bitcast(F32),
                                      ALU.subtract).then_inc(kvb_lo_ready, 1)

                def group(g, s):
                    for t in range(TT):
                        low_kv(g, t)
                    head_blocks(g, s)

                norm(0)
                dve.wait_ge(o_done, b * 16 + 2)
                dve.memset(kv_hi[:, :, 256:258].bitcast(F32), 1.0).then_inc(ones_set, 1)
                dve.memset(kv_lo[:, :, 256:258].bitcast(F32), 0.0).then_inc(ones_set, 1)
                for t in range(TT):
                    if t < TT - 1:
                        norm(t + 1)
                    low_xt(t)
                    if t:
                        low_kv(0, t - 1)
                low_kv(0, TT - 1)
                head_blocks(0, 0)
                with dve.Fori(0, KT // 2 - 1) as i:
                    group(i * 2 + 1, 1)
                    group(i * 2 + 2, 0)
                group(KT - 1, 1)

                def attend(u):
                    dve.wait_ge(o_done, b * 16 + u + 2)
                    dve.wait_ge(nd_done, b * 16 + u + 1 + 2)
                    dve.tensor_scalar(rden[:], pair[2 + u % 2][:, 1, :], ATT_EPS, None, ALU.add).then_inc(rden_step, 1)
                    dve.wait_ge(rden_step, (b * 16 + u) * 2 + 1)
                    dve.reciprocal(rden[:], rden[:]).then_inc(rden_step, 1)
                    dve.wait_ge(rden_step, (b * 16 + u) * 2 + 2)
                    dve.tensor_tensor(o[:, u // 2, u % 2 * HALF:u % 2 * HALF + HALF], pair[2 + u % 2][:, 0, :], rden[:],
                                      ALU.mult).then_inc(o_done, 1)

                for u in range(16):
                    dve.wait_ge(q_hi_ready, b * 16 + u + 1)
                    dve.scalar_tensor_tensor(q_lo[:, u % 2, :], pair[u % 4 // 2][:, u % 2, :], 0.0,
                                             q_hi[:, u % 2, :].bitcast(F32), ALU.max, ALU.subtract).then_inc(q_lo_ready, 1)
                    if u:
                        attend(u - 1)
                attend(15)
                for j in (1, 3):
                    dve.wait_ge(w_hi_ready, b * 16 + 12 + j + 1)
                    cols = slice(j * 256, j * 256 + 256)
                    dve.tensor_tensor(act_lo[:, :, cols], w_view(w_raw, j % 2), act_hi[:, :, cols].bitcast(F32),
                                      ALU.subtract).then_inc(wp_lo_dve, 1)

                def low_o(t):
                    s = t % 2
                    dve.wait_ge(os_hi_ready, b * 8 + t + 1)
                    dve.tensor_tensor(o_view(w_lo, s), o[:, :, t * P:(t + 1) * P], o_view(w_hi, s).bitcast(F32),
                                      ALU.subtract).then_inc(os_lo_ready, 1)

                low_o(0)
                for t in range(TT):
                    s = t % 2
                    if t < TT - 1:
                        low_o(t + 1)
                    dve.wait_ge(proj_done, b * 8 + t + 1 + 2)
                    dve.wait_ge(xb_ready, b * 8 + t + 1)
                    dve.tensor_tensor(x_tok[:, s, :], pair[s][:].rearrange("p a n -> p (a n)"), x_tok[:, s, :],
                                      ALU.add).then_inc(x1_ready, 1)
                    dve.wait_ge(x1_ready, b * 8 + t + 1 + 2)
                    dve.wait_ge(tr_done, b * 16 + 8 + t + 1)
                    layer_norm(dve, x_tok[:, s, :], xn[:, s, :], b * 16 + 8 + t).then_inc(xn_ready, 1)

        @block.gpsimd
        def _(pool):
            pool.sem_inc(w_lo_ready, 2)
            pool.memset(minus_half[:], -0.5).then_inc(half_set, 1)
            pool.wait_ge(half_set, 1)
            pool.wait_ge(const_in, 48)

            def low_weights(b, i, s):
                pool.wait_ge(w_hi_ready, b * 16 + i * 2 + s + 1)
                pool.tensor_tensor(w_lo[:, s, :], w_raw[:, s, :], w_hi[:, s, :].bitcast(F32),
                                   ALU.subtract).then_inc(w_lo_ready, 1)

            def inverse_deviation(n):
                pool.wait_ge(var_ready, n + 1)
                pool.tensor_tensor(rstd[:], var_eps[:], minus_half[:], ALU.pow).then_inc(rstd_ready, 1)

            with pool.Fori(0, B) as b:
                for s in range(2):
                    low_weights(b, 0, s)
                with pool.Fori(0, TT) as t:
                    inverse_deviation(b * 16 + t)
                with pool.Fori(1, 6) as i:
                    for s in range(2):
                        low_weights(b, i, s)
                for j in range(4):
                    pool.wait_ge(w_hi_ready, b * 16 + 12 + j + 1)
                    cols = slice(j * 256, j * 256 + 256)
                    if j % 2 == 0:
                        pool.tensor_tensor(act_lo[:, :, cols], w_view(w_raw, j % 2), act_hi[:, :, cols].bitcast(F32),
                                           ALU.subtract).then_inc(w_lo_ready, 1)
                    else:
                        pool.wait_ge(w_lo_ready, b * 16 + 12 + j + 2)
                        pool.wait_ge(wp_lo_dve, b * 2 + j // 2 + 1)
                        pool.sem_inc(w_lo_ready, 1)
                for t in range(TT):
                    s = t % 2
                    pool.wait_ge(x_loaded[s], b * 128 + 64 + t // 2 * 16 + 16)
                    pool.tensor_tensor(x_tok[:, s, :], x_tok[:, s, :], bias[:], ALU.add).then_inc(xb_ready, 1)
                    inverse_deviation(b * 16 + 8 + t)

        @block.scalar
        def _(act):
            act.sem_inc(kt_evac, 2)
            for s in range(2):
                act.sem_inc(kt_stored[s], 16)

            def high_weights(b, i, s):
                act.wait_ge(raw_loaded[s], b * 128 + i * 16 + 16)
                act.activation(w_hi[:, s, :], w_raw[:, s, :], ACT.Copy).then_inc(w_hi_ready, 1)

            with act.Fori(0, B) as b:
                act.wait_ge(proj_done, b * 8 + 2)
                for s in range(2):
                    high_weights(b, 0, s)
                def high_xt(t):
                    act.wait_ge(tr_done, b * 16 + t + 1 + 2)
                    act.activation(act_hi[:, :, t * P:(t + 1) * P], pair[3][:].rearrange("p a (k t) -> p (a k) t", t=P),
                                   ACT.Copy).then_inc(xt_hi, 1)

                def high_kv(g, t):
                    bank = pair[t % 4 // 2][:, t % 2, :]
                    act.wait_ge(kv_main, (b * 8 + g) * 8 + t + 1)
                    if t < TT - 1:
                        act.wait_ge(kv_free, (b * 8 + g) * 7 + t + 1)
                    else:
                        act.wait_ge(vk_done, b * 8 + g + 1)
                    act.activation(kv_hi[:, t, 0:P], bank[:, 0:P], ACT.Relu)
                    act.activation(kv_hi[:, t, P:2 * P], bank[:, P:2 * P], ACT.Copy).then_inc(kv_hi_ready, 1)

                def head_blocks_high(g):
                    act.wait_ge(kvb_made, (b * 8 + g) * 2 + 2 + 4)
                    act.activation(kvb_hi[:, ds(g, 1), :].rearrange("p a n -> p (a n)"), kvb[:],
                                   ACT.Copy).then_inc(kvb_hi_ready, 1)

                def group(g, s, i):
                    for t in range(TT):
                        high_kv(g, t)
                    head_blocks_high(g)
                    high_weights(b, i, s)

                for t in range(TT):
                    high_xt(t)
                    if t:
                        high_kv(0, t - 1)
                high_kv(0, TT - 1)
                head_blocks_high(0)
                high_weights(b, 1, 0)
                with act.Fori(0, KT // 2 - 1) as i:
                    group(i * 2 + 1, 1, i + 1)
                    group(i * 2 + 2, 0, i + 2)
                group(KT - 1, 1, KT // 2)
                for u in range(16):
                    act.wait_ge(q_main, b * 16 + u + 1)
                    act.wait_ge(nd_done, b * 16 + u + 1)
                    act.activation(q_hi[:, u % 2, :], pair[u % 4 // 2][:, u % 2, :], ACT.Relu).then_inc(q_hi_ready, 1)
                    if u in (4, 8):
                        high_weights(b, 5, u // 4 - 1)
                with act.Fori(0, 2) as i:
                    for s in range(2):
                        act.wait_ge(raw_loaded[s], b * 128 + 96 + i * 16 + 16)
                        act.activation(act_hi[:, :, ds((i * 2 + s) * 256, 256)], w_view(w_raw, s),
                                       ACT.Copy).then_inc(w_hi_ready, 1)

                def high_o(t):
                    s = t % 2
                    act.wait_ge(o_done, b * 16 + (15 if t < TT // 2 else 16) + 2)
                    act.wait_ge(proj_done, b * 8 + t + 1)
                    act.activation(o_view(w_hi, s), o[:, :, t * P:(t + 1) * P], ACT.Copy).then_inc(os_hi_ready, 1)

                def turned_k(t):
                    s = t % 2
                    act.wait_ge(tr_done, b * 16 + 8 + t + 1 + 2)
                    act.wait_ge(kt_stored[s], b * 64 + t // 2 * 16 + 16)
                    act.activation(kT[:, s, :, :], pair[2 + s][:].rearrange("p a (k t) -> p (a k) t", t=P),
                                   ACT.Copy).then_inc(kt_evac, 1)
                    act.wait_ge(kt_evac, b * 8 + t + 1 + 2)
                    act.dma_start(kT_dram[ds(b * C, C), t * P:(t + 1) * P].rearrange("(k c) t -> c k t", c=P),
                                  kT[:, s, :, :]).then_inc(kt_stored[s], 16)

                high_o(0)
                high_o(1)
                for t in range(TT):
                    if t:
                        turned_k(t - 1)
                    if t + 2 < TT:
                        high_o(t + 2)
                turned_k(TT - 1)
            for s in range(2):
                act.wait_ge(kt_stored[s], B * 64 + 16)

        @block.tensor
        def _(pe):
            pe.sem_inc(tr_done, 2)
            pe.sem_inc(kv_free, TT - 1)
            pe.sem_inc(nd_done, 2)
            pe.sem_inc(proj_done, 2)
            pe.sem_inc(vk_done, 1)
            pe.wait_ge(const_in, 48)
            with pe.Fori(0, B) as b:
                def turn_xn(t):
                    pe.wait_ge(xn_ready, b * 16 + t + 1 + 2)
                    pe.wait_ge(xt_lo, b * 8 + t + 2)
                    for k in range(KT):
                        mm = pe.transpose(pair[3][:, k // 4, k % 4 * P:k % 4 * P + P],
                                          xn[:, t % 2, k * P:(k + 1) * P], ident[:])
                    mm.then_inc(tr_done, 1)

                def k_and_v(g, s, t):
                    pe.wait_ge(kv_lo_ready, (b * 8 + g) * 8 + t + 1)
                    for k in range(KT):
                        mm = product3(pe, pair[t % 4 // 2][:, t % 2, 0:256],
                                      act_hi[:, k, t * P:(t + 1) * P], act_lo[:, k, t * P:(t + 1) * P],
                                      w_view(w_hi, s)[:, k, :], w_view(w_lo, s)[:, k, :], k == 0, k == KT - 1)
                    mm.then_inc(kv_main, 1)

                def k_times_v(g, s, t):
                    pe.wait_ge(kv_lo_ready, (b * 8 + g) * 8 + t + 1 + 4)
                    mm = product3(pe, pair[2][:, s, 0:130], kv_hi[:, t, 0:P], kv_lo[:, t, 0:P],
                                  kv_hi[:, t, P:258], kv_lo[:, t, P:258], t == 0, t == TT - 1)
                    mm.then_inc(vk_done if t == TT - 1 else kv_free, 1)

                def group_start(g):
                    pe.wait_ge(w_lo_ready, b * 16 + g + 1 + 2)
                    pe.wait_ge(kvb_made, (b * 8 + g) * 2 + 2)

                def group(g, s):
                    group_start(g)
                    for t in range(TT):
                        k_and_v(g, s, t)
                        if t:
                            k_times_v(g, s, t - 1)
                    k_times_v(g, s, TT - 1)

                pe.wait_ge(kt_evac, b * 8 + 2)
                turn_xn(0)
                group_start(0)
                pe.wait_ge(ones_set, b * 2 + 2)
                for t in range(TT):
                    if t < TT - 1:
                        turn_xn(t + 1)
                    pe.wait_ge(xt_lo, b * 8 + t + 1 + 2)
                    k_and_v(0, 0, t)
                    if t:
                        k_times_v(0, 0, t - 1)
                k_times_v(0, 0, TT - 1)
                with pe.Fori(0, KT // 2 - 1) as i:
                    group(i * 2 + 1, 1)
                    group(i * 2 + 2, 0)
                group(KT - 1, 1)

                def numerator_denominator(u):
                    c = u // 2
                    pe.wait_ge(q_lo_ready, b * 16 + u + 1 + 4)
                    pe.wait_ge(o_done, b * 16 + u + 1)
                    for h in range(2):
                        mm = product3(pe, pair[2 + u % 2][:, h, :], kvb_hi[:, c, h * P:(h + 1) * P], kvb_lo[:, c, h * P:(h + 1) * P],
                                      q_hi[:, u % 2, :], q_lo[:, u % 2, :], True, True)
                    mm.then_inc(nd_done, 1)

                for u in range(16):
                    c, h = u // 2, u % 2
                    s = c // 2 % 2
                    if u % 4 == 0:
                        pe.wait_ge(w_lo_ready, b * 16 + 8 + c // 2 + 1 + 2)
                    pe.wait_ge(q_lo_ready, b * 16 + u + 1)
                    for k in range(KT):
                        mm = product3(pe, pair[u % 4 // 2][:, u % 2, :],
                                      w_view(w_hi, s)[:, k, c % 2 * P:c % 2 * P + P], w_view(w_lo, s)[:, k, c % 2 * P:c % 2 * P + P],
                                      act_hi[:, k, h * HALF:(h + 1) * HALF], act_lo[:, k, h * HALF:(h + 1) * HALF],
                                      k == 0, k == KT - 1)
                    mm.then_inc(q_main, 1)
                    if u == 0:
                        pe.wait_ge(kvb_lo_ready, b * 8 + 8 + 1)
                    if u:
                        numerator_denominator(u - 1)
                numerator_denominator(15)

                def project(t):
                    s = t % 2
                    pe.wait_ge(os_lo_ready, b * 8 + t + 1)
                    pe.wait_ge(x1_ready, b * 8 + t + 1)
                    for h in range(2):
                        if t == 0:
                            pe.wait_ge(w_lo_ready, b * 16 + 14 + h * 2 + 2)
                        for k in range(KT):
                            mm = product3(pe, pair[s][:, h, :], o_view(w_hi, s)[:, k, :], o_view(w_lo, s)[:, k, :],
                                          act_hi[:, k, h * HALF:(h + 1) * HALF], act_lo[:, k, h * HALF:(h + 1) * HALF],
                                          k == 0, k == KT - 1)
                    mm.then_inc(proj_done, 1)

                def turn_k(t):
                    s = t % 2
                    pe.wait_ge(xn_ready, b * 16 + 8 + t + 1 + 2)
                    pe.wait_ge(kt_evac, b * 8 + t + 1)
                    for k in range(KT):
                        mm = pe.transpose(pair[2 + s][:, k // 4, k % 4 * P:k % 4 * P + P],
                                          xn[:, s, k * P:(k + 1) * P], ident[:])
                    mm.then_inc(tr_done, 1)

                for t in range(TT):
                    project(t)
                    if t:
                        turn_k(t - 1)
                turn_k(TT - 1)


def wkv_phase(nc, kT_dram, ctxT, w_in, u_in, ident_in, y_dram):
    with ExitStack() as ctx:
        m = Tools(nc, ctx, "wkv")
        k = m.sb("k", [P, 2, T])
        v = m.sb("v", [P, 2, T])
        top = m.sb("top", [P, T + 1])
        p = m.sb("p", [P, T + 1])
        q = m.sb("q", [P, T + 1])
        decay = m.sb("decay", [P, 2, T])
        new = m.sb("new", [P, 2, T])
        own = m.sb("own", [P, 2, T])
        new_v = m.sb("new_v", [P, T])
        own_v = m.sb("own_v", [P, 2, T])
        num = m.sb("num", [P, T])
        den = m.sb("den", [P, T])
        y = m.sb("y", [P, 2, T])
        y_tok = m.sb("y_tok", [P, 2, TT, P])
        w_col = m.sb("w_col", [P, KT])
        u_col = m.sb("u_col", [P, KT])
        ident = m.sb("ident", [P, P])
        y_ps = [m.ps(f"y_ps{s}", [P, 2, HALF]) for s in range(2)]
        const_in = m.sem("const_in")
        start_set = m.sem("start_set")
        k_loaded = [m.sem(f"k_loaded{s}") for s in range(2)]
        top_ready, logs_ready, own_log = m.sem("top_ready"), m.sem("logs_ready"), m.sem("own_log")
        exps_ready, new_v_ready = m.sem("exps_ready"), m.sem("new_v_ready")
        own_v_ready, state_ready = m.sem("own_v_ready"), m.sem("state_ready")
        sum_ready, y_ready = m.sem("sum_ready"), m.sem("y_ready")
        y_turned, y_evac = m.sem("y_turned"), m.sem("y_evac")
        y_stored = [m.sem(f"y_stored{s}") for s in range(2)]
        held = {e: m.sem(f"held_{e}") for e in ("sp", "act", "pool", "pe", "dve")}
        block = ctx.enter_context(nc.Block())
        N = B * KT

        @block.sync
        def _(sp):
            sp.dma_start(ident[:], ident_in).then_inc(const_in, 16)
            sp.dma_start(w_col[:], w_in).then_inc(const_in, 16)
            sp.dma_start(u_col[:], u_in).then_inc(const_in, 16)
            with sp.Fori(0, N // 2) as i:
                for s in range(2):
                    sp.wait_ge(y_ready, i * 2 + s + 1)
                    sp.dma_start(k[:, s, :], kT_dram[ds((i * 2 + s) * P, P), :]).then_inc(k_loaded[s], 16)
                    sp.dma_start(v[:, s, :], ctxT[ds((i * 2 + s) * P, P), :]).then_inc(k_loaded[s], 16)

        @block.gpsimd
        def _(pool):
            pool.sem_inc(logs_ready, 1)
            with pool.Fori(0, N // 2) as i:
                for s in range(2):
                    n = i * 2 + s
                    pool.wait_ge(exps_ready, n * 3 + 1)
                    pool.wait_ge(top_ready, n + 1)
                    pool.tensor_tensor(decay[:, s, :], top[:, 0:T], top[:, 1:T + 1], ALU.subtract).then_inc(logs_ready, 1)
                    pool.wait_ge(exps_ready, n * 3 + 3 + 1)
                    pool.wait_ge(y_ready, n + 1)
                    pool.tensor_tensor(own_v[:, s, :], own[:, s, :], v[:, s, :], ALU.mult).then_inc(own_v_ready, 1)

        @block.scalar
        def _(act):
            act.sem_inc(exps_ready, 1)
            act.sem_inc(y_evac, 1)
            for s in range(2):
                act.sem_inc(y_stored[s], 16)
            act.wait_ge(const_in, 48)
            with act.Fori(0, B) as b:
                for c in range(KT):
                    s = c % 2
                    n = b * KT + c
                    act.wait_ge(own_log, n * 4 + 4 + 1)
                    act.activation(new[:, s, :], new[:, s, :], ACT.Exp).then_inc(exps_ready, 1)
                    act.wait_ge(logs_ready, n + 1 + 1)
                    act.activation(decay[:, s, :], decay[:, s, :], ACT.Exp, bias=w_col[:, c:c + 1]).then_inc(exps_ready, 1)
                    act.activation(own[:, s, :], own[:, s, :], ACT.Exp).then_inc(exps_ready, 1)
                    act.wait_ge(y_turned, n + 1 + 1)
                    act.wait_ge(y_stored[s], b * 64 + c // 2 * 16 + 16)
                    act.activation(y_tok[:, s, :, :], y_ps[s][:].rearrange("p a (t c) -> p (a t) c", c=P),
                                   ACT.Copy).then_inc(y_evac, 1)
                    act.wait_ge(y_evac, n + 1 + 1)
                    act.dma_start(y_dram[ds(b * T, T), c * P:(c + 1) * P].rearrange("(t p) c -> p t c", p=P),
                                  y_tok[:, s, :, :]).then_inc(y_stored[s], 16)
            for s in range(2):
                act.wait_ge(y_stored[s], B * 64 + 16)

        @block.vector
        def _(dve):
            dve.sem_inc(y_ready, 2)
            dve.sem_inc(own_log, 1)
            dve.wait_ge(const_in, 48)
            dve.memset(top[:, 0:1], NO_PAST).then_inc(start_set, 1)
            dve.memset(p[:, 0:1], 0.0).then_inc(start_set, 1)
            dve.memset(q[:, 0:1], 0.0).then_inc(start_set, 1)
            dve.wait_ge(start_set, 3)
            with dve.Fori(0, B) as b:
                for c in range(KT):
                    s = c % 2
                    n = b * KT + c
                    dve.wait_ge(k_loaded[s], b * 128 + c // 2 * 32 + 32)
                    dve.wait_ge(logs_ready, n + 1)
                    dve.wait_ge(own_log, n * 4 + 1)
                    dve.tensor_tensor_scan(top[:, 1:T + 1], w_col[:, c:c + 1].to_broadcast([P, T]), k[:, s, :],
                                           NO_PAST, ALU.add, ALU.max).then_inc(top_ready, 1)
                    dve.wait_ge(top_ready, n + 1)
                    dve.tensor_tensor(new[:, s, :], k[:, s, :], top[:, 1:T + 1], ALU.subtract).then_inc(own_log, 1)
                    dve.tensor_tensor(own[:, s, :], k[:, s, :], top[:, 0:T], ALU.subtract).then_inc(own_log, 1)
                    dve.wait_ge(own_log, n * 4 + 2 + 1)
                    dve.tensor_scalar(own[:, s, :], own[:, s, :], u_col[:, c:c + 1], R_CLAMP, ALU.add, ALU.min).then_inc(own_log, 2)
                    dve.wait_ge(exps_ready, n * 3 + 1 + 1)
                    dve.tensor_tensor(new_v[:], new[:, s, :], v[:, s, :], ALU.mult).then_inc(new_v_ready, 1)
                    dve.wait_ge(exps_ready, n * 3 + 2 + 1)
                    dve.wait_ge(new_v_ready, n + 1)
                    dve.tensor_tensor_scan(q[:, 1:T + 1], decay[:, s, :], new[:, s, :], 0.0, ALU.mult, ALU.add).then_inc(state_ready, 1)
                    dve.tensor_tensor_scan(p[:, 1:T + 1], decay[:, s, :], new_v[:], 0.0, ALU.mult, ALU.add).then_inc(state_ready, 1)
                    dve.wait_ge(exps_ready, n * 3 + 3 + 1)
                    dve.wait_ge(state_ready, n * 2 + 2)
                    dve.wait_ge(y_ready, n + 2)
                    dve.tensor_tensor(den[:], own[:, s, :], q[:, 0:T], ALU.add).then_inc(sum_ready, 1)
                    dve.wait_ge(own_v_ready, n + 1)
                    dve.tensor_tensor(num[:], own_v[:, s, :], p[:, 0:T], ALU.add).then_inc(sum_ready, 1)
                    dve.wait_ge(sum_ready, n * 3 + 2)
                    dve.reciprocal(den[:], den[:]).then_inc(sum_ready, 1)
                    dve.wait_ge(sum_ready, n * 3 + 3)
                    if c >= 2:
                        dve.wait_ge(y_turned, b * KT + c - 1 + 1)
                    else:
                        dve.wait_ge(y_turned, b * KT + 1)
                    dve.tensor_tensor(y[:, s, :], num[:], den[:], ALU.mult).then_inc(y_ready, 1)

        @block.tensor
        def _(pe):
            pe.sem_inc(y_turned, 1)
            pe.wait_ge(const_in, 48)
            with pe.Fori(0, B) as b:
                for c in range(KT):
                    s = c % 2
                    n = b * KT + c
                    pe.wait_ge(y_ready, n + 1 + 2)
                    if c >= 2:
                        pe.wait_ge(y_evac, b * KT + c - 1 + 1)
                    else:
                        pe.wait_ge(y_evac, b * KT + 1)
                    for t in range(TT):
                        mm = pe.transpose(y_ps[s][:, t // 4, t % 4 * P:t % 4 * P + P], y[:, s, t * P:(t + 1) * P], ident[:])
                    mm.then_inc(y_turned, 1)


def select_phase(nc, x1_dram, y_dram, wr_in, br_in, tri_in, tok_in, score_dram, sel_dram, out):
    with ExitStack() as ctx:
        m = Tools(nc, ctx, "sel")
        x2 = m.sb("x2", [P, TT, C + 1])
        y = m.sb("y", [P, 2, C])
        xn = m.sb("xn", [P, C])
        w_r = m.sb("w_r", [P, C])
        b_r = m.sb("b_r", [P, 1])
        earlier = m.sb("earlier", [P, TT, T])
        tok = m.sb("tok", [P, TT])
        base = m.sb("base", [P, 1])
        tok_f = m.sb("tok_f", [P, TT])
        score = m.sb("score", [P, TT])
        row = m.sb("row", [P, T])
        scrap = m.sb("scrap", [P, T])
        above = m.sb("above", [P, TT])
        tied = m.sb("tied", [P, TT])
        rank = m.sb("rank", [P, TT])
        rank_i = m.sb("rank_i", [P, TT], I32)
        stats = m.sb("stats", [P, 2, 6])
        mv = m.sb("mv", [P, 2])
        var_eps = m.sb("var_eps", [P, 1])
        minus_half = m.sb("minus_half", [P, 1])
        rstd = m.sb("rstd", [P, 1])
        const_in = m.sem("const_in")
        x_loaded = [m.sem(f"x_loaded{s}") for s in range(2)]
        y_free, x2_ready, step, x2_stored = m.sem("y_free"), m.sem("x2_ready"), m.sem("step"), m.sem("x2_stored")
        score_ready, score_stored, row_loaded = m.sem("score_ready"), m.sem("score_stored"), m.sem("row_loaded")
        counted, rank_ready = m.sem("counted"), m.sem("rank_ready")
        scattered, rows_left = m.sem("scattered"), m.sem("rows_left")
        base_step, var_ready, rstd_ready, half_set = m.sem("base_step"), m.sem("var_ready"), m.sem("rstd_ready"), m.sem("half_set")
        held = {e: m.sem(f"held_{e}") for e in ("sp", "act", "pool", "pe", "dve")}
        block = ctx.enter_context(nc.Block())

        @block.sync
        def _(sp):
            sp.dma_start(w_r[:], wr_in.rearrange("(a n) -> a n", a=1).to_broadcast([P, C])).then_inc(const_in, 16)
            sp.dma_start(b_r[:], br_in.rearrange("(a n) -> a n", a=1).to_broadcast([P, 1])).then_inc(const_in, 16)
            sp.dma_start(earlier[:].rearrange("p t c -> p (t c)"), tri_in).then_inc(const_in, 16)
            sp.dma_start(tok[:], tok_in).then_inc(const_in, 16)
            with sp.Fori(0, B) as b:
                sp.wait_ge(rows_left, b + 1)
                hold(sp, x2_stored, b * 128 + 16, held["sp"])
                with sp.Fori(0, TT // 2) as i:
                    for s in range(2):
                        t = i * 2 + s
                        rows = ds(b * T + t * P, P)
                        sp.wait_ge(x2_ready, b * 8 + t + 1)
                        sp.dma_start(x2[:, ds(t, 1), 0:C].rearrange("p a n -> p (a n)"), x1_dram[rows, :]).then_inc(x_loaded[s], 16)
                        sp.dma_start(y[:, s, :], y_dram[rows, :]).then_inc(x_loaded[s], 16)
                sp.wait_ge(score_ready, b + 1)
                sp.dma_start(score_dram[ds(b * T, T)].rearrange("(p t) -> p t", p=P), score[:]).then_inc(score_stored, 16)
                sp.wait_ge(score_stored, b * 16 + 16)
                sp.dma_start(row[:], score_dram[ds(b * T, T)].rearrange("(a n) -> a n", a=1).to_broadcast([P, T])).then_inc(row_loaded, 16)

        @block.scalar
        def _(act):
            act.sem_inc(x2_stored, 16)
            with act.Fori(0, B) as b:
                with act.Fori(0, TT) as t:
                    act.wait_ge(x2_ready, b * 8 + t + 1 + 2)
                    act.dma_start(out[ds(b * T + t * P, P), :], x2[:, ds(t, 1), 0:C].rearrange("p a n -> p (a n)")).then_inc(x2_stored, 16)
            act.wait_ge(x2_stored, B * 128 + 16)

        @block.vector
        def _(dve):
            dve.sem_inc(x2_ready, 2)
            dve.sem_inc(counted, 1)
            dve.wait_ge(const_in, 64)
            dve.memset(base[:], 0.0).then_inc(base_step, 1)
            with dve.Fori(0, B) as b:
                dve.wait_ge(base_step, b * 2 + 1)
                dve.tensor_scalar(tok_f[:], tok[:], base[:, 0:1], None, ALU.add).then_inc(base_step, 1)
                dve.wait_ge(base_step, b * 2 + 2)
                for t in range(TT):
                    s = t % 2
                    first = (b * 8 + t) * 4
                    here = x2[:, t, 0:C]
                    dve.wait_ge(x_loaded[s], b * 128 + t // 2 * 32 + 32)
                    dve.tensor_copy(x2[:, t, C:C + 1].bitcast(I32), tok_f[:, t:t + 1])
                    dve.tensor_tensor(here, here, y[:, s, :], ALU.add).then_inc(x2_ready, 1)
                    dve.wait_ge(x2_ready, b * 8 + t + 1 + 2)
                    for h in range(2):
                        dve.bn_stats(stats[:, h, :], x2[:, t, h * HALF:(h + 1) * HALF]).then_inc(step, 1)
                    hold(dve, step, first + 2, held["dve"])
                    dve.bn_aggr(mv[:], stats[:]).then_inc(step, 1)
                    dve.wait_ge(step, first + 3)
                    dve.tensor_scalar(var_eps[:], mv[:, 1:2], LN_EPS, None, ALU.add).then_inc(var_ready, 1)
                    dve.wait_ge(rstd_ready, b * 8 + t + 1)
                    dve.wait_ge(counted, b * 24 + t + 1)
                    dve.tensor_scalar(xn[:], here, mv[:, 0:1], rstd[:, 0:1], ALU.subtract, ALU.mult).then_inc(step, 1)
                    dve.wait_ge(step, first + 4)
                    dve.tensor_tensor_reduce(scrap[:], xn[:], w_r[:], 1.0, 0.0, ALU.mult, ALU.add,
                                             rank[:, t:t + 1]).then_inc(counted, 1)
                dve.wait_ge(counted, b * 24 + 8 + 1)
                dve.tensor_scalar(score[:], rank[:], b_r[:, 0:1], None, ALU.add).then_inc(score_ready, 1)
                dve.wait_ge(score_ready, b + 1)
                dve.wait_ge(row_loaded, b * 16 + 16)
                for t in range(TT):
                    dve.wait_ge(counted, b * 24 + 8 + t * 2 + 1)
                    dve.tensor_scalar(scrap[:], row[:], score[:, t:t + 1], None, ALU.is_gt, ALU.add,
                                      accum_out=above[:, t:t + 1]).then_inc(counted, 1)
                    dve.wait_ge(counted, b * 24 + 9 + t * 2 + 1)
                    dve.scalar_tensor_tensor(scrap[:], row[:], score[:, t:t + 1], earlier[:, t, :],
                                             ALU.is_equal, ALU.mult, accum_out=tied[:, t:t + 1]).then_inc(counted, 1)
                dve.wait_ge(counted, b * 24 + 24 + 1)
                dve.tensor_tensor(above[:], above[:], tied[:], ALU.add).then_inc(rank_ready, 1)
                dve.wait_ge(rank_ready, b * 2 + 1)
                dve.wait_ge(rows_left, b + 1)
                dve.tensor_scalar(rank_i[:], above[:], base[:, 0:1], None, ALU.add).then_inc(rank_ready, 1)
                dve.wait_ge(rank_ready, b * 2 + 2)
                dve.tensor_scalar(base[:], base[:], float(T), None, ALU.add).then_inc(base_step, 1)

        @block.gpsimd
        def _(pool):
            pool.sem_inc(rows_left, 1)
            pool.memset(minus_half[:], -0.5).then_inc(half_set, 1)
            pool.wait_ge(half_set, 1)
            with pool.Fori(0, B) as b:
                with pool.Fori(0, TT) as t:
                    pool.wait_ge(var_ready, b * 8 + t + 1)
                    pool.tensor_tensor(rstd[:], var_eps[:], minus_half[:], ALU.pow).then_inc(rstd_ready, 1)
                hold(pool, rank_ready, b * 2 + 2, held["pool"])
                for t in range(TT):
                    pool.indirect_dma_start(sel_dram, bass.IndirectOffsetOnAxis(rank_i[:, t:t + 1], 0),
                                            x2[:, t, :], None).then_inc(scattered, 16)
                hold(pool, scattered, b * 128 + 128, rows_left)


def ffn_phase(nc, sel_dram, w1, b1_in, w2, b2_in, ident_in, out):
    ST = SEL // P
    FT = CHUNK // P
    with ExitStack() as ctx:
        m = Tools(nc, ctx, "ffn")
        x2 = m.sb("x2", [P, ST, C + 1])
        xn = m.sb("xn", [P, 2, C])
        xT_hi = m.sb("xT_hi", [P, KT, SEL], F32R)
        xT_lo = m.sb("xT_lo", [P, KT, SEL], F32R)
        w_raw = m.sb("w_raw", [P, 2, 4096])
        w1_hi = m.sb("w1_hi", [P, KT, CHUNK], F32R)
        w1_lo = m.sb("w1_lo", [P, KT, CHUNK], F32R)
        w2_hi = m.sb("w2_hi", [P, FT, C], F32R)
        w2_lo = m.sb("w2_lo", [P, FT, C], F32R)
        h = m.sb("h", [P, 2, SEL])
        h_hi = m.sb("h_hi", [P, FT, SEL], F32R)
        h_lo = m.sb("h_lo", [P, FT, SEL], F32R)
        acc = m.sb("acc", [P, ST, C])
        b1 = m.sb("b1", [P, DF // P])
        b2 = m.sb("b2", [P, C])
        ident = m.sb("ident", [P, P])
        stats = m.sb("stats", [P, 2, 6])
        mv = m.sb("mv", [P, 2])
        var_eps = m.sb("var_eps", [P, 1])
        minus_half = m.sb("minus_half", [P, 1])
        rstd = m.sb("rstd", [P, 1])
        h_ps = [m.ps(f"h_ps{s}", [P, 2, HALF]) for s in range(2)]
        o_ps = [m.ps(f"o_ps{s}", [P, 2, HALF]) for s in range(2)]
        const_in, x_loaded, step = m.sem("const_in"), m.sem("x_loaded"), m.sem("step")
        xn_ready, tr_done, xt_hi, xt_lo = m.sem("xn_ready"), m.sem("tr_done"), m.sem("xt_hi"), m.sem("xt_lo")
        w1_loaded, w1_hi_ready, w1_lo_ready = m.sem("w1_loaded"), m.sem("w1_hi_ready"), m.sem("w1_lo_ready")
        w2_loaded, w2_hi_ready, w2_lo_ready = m.sem("w2_loaded"), m.sem("w2_hi_ready"), m.sem("w2_lo_ready")
        up_done, h_ready, h_hi_ready, h_lo_ready = m.sem("up_done"), m.sem("h_ready"), m.sem("h_hi_ready"), m.sem("h_lo_ready")
        down_done, added, acc_set = m.sem("down_done"), m.sem("added"), m.sem("acc_set")
        final_ready, rows_stored, rows_left = m.sem("final_ready"), m.sem("rows_stored"), m.sem("rows_left")
        var_ready, rstd_ready, half_set = m.sem("var_ready"), m.sem("rstd_ready"), m.sem("half_set")
        held = {e: m.sem(f"held_{e}") for e in ("sp", "act", "pool", "pe", "dve")}
        block = ctx.enter_context(nc.Block())

        @block.sync
        def _(sp):
            sp.dma_start(ident[:], ident_in).then_inc(const_in, 16)
            sp.dma_start(b1[:], b1_in).then_inc(const_in, 16)
            sp.dma_start(b2[:], b2_in.rearrange("(a n) -> a n", a=1).to_broadcast([P, C])).then_inc(const_in, 16)
            with sp.Fori(0, B) as b:
                sp.wait_ge(rows_left, b + 1)
                sp.dma_start(x2[:], sel_dram[ds(b * T, SEL), :].rearrange("(t p) c -> p t c", p=P)).then_inc(x_loaded, 16)
                with sp.Fori(0, STEPS) as j:
                    sp.wait_ge(w1_lo_ready, b * STEPS + j + 1)
                    sp.dma_start(w_raw[:, 0, :], w1[ds(j * P, P), :]).then_inc(w1_loaded, 16)
                    sp.wait_ge(w2_lo_ready, b * STEPS + j + 1)
                    sp.dma_start(w_raw[:, 1, :].rearrange("p (f n) -> p f n", f=FT),
                                 w2[ds(j * CHUNK, CHUNK), :].rearrange("(f p) n -> p f n", p=P)).then_inc(w2_loaded, 16)

        @block.gpsimd
        def _(pool):
            pool.sem_inc(rows_left, 1)
            pool.sem_inc(w1_lo_ready, 1)
            pool.sem_inc(w2_lo_ready, 1)
            pool.memset(minus_half[:], -0.5).then_inc(half_set, 1)
            pool.wait_ge(half_set, 1)
            with pool.Fori(0, B) as b:
                with pool.Fori(0, ST) as t:
                    pool.wait_ge(var_ready, b * 4 + t + 1)
                    pool.tensor_tensor(rstd[:], var_eps[:], minus_half[:], ALU.pow).then_inc(rstd_ready, 1)
                with pool.Fori(0, STEPS) as j:
                    n = b * STEPS + j
                    pool.wait_ge(w1_hi_ready, n + 1)
                    pool.tensor_tensor(w1_lo[:].rearrange("p k n -> p (k n)"), w_raw[:, 0, :],
                                       w1_hi[:].rearrange("p k n -> p (k n)").bitcast(F32), ALU.subtract).then_inc(w1_lo_ready, 1)
                    pool.wait_ge(w2_hi_ready, n + 1)
                    pool.tensor_tensor(w2_lo[:].rearrange("p k n -> p (k n)"), w_raw[:, 1, :],
                                       w2_hi[:].rearrange("p k n -> p (k n)").bitcast(F32), ALU.subtract).then_inc(w2_lo_ready, 1)
                hold(pool, final_ready, b * 4 + 4, held["pool"])
                for t in range(ST):
                    pool.indirect_dma_start(out, bass.IndirectOffsetOnAxis(x2[:, t, C:C + 1].bitcast(I32), 0),
                                            acc[:, t, :], None).then_inc(rows_stored, 16)
                hold(pool, rows_stored, b * 64 + 64, rows_left)

        @block.scalar
        def _(act):
            act.wait_ge(const_in, 48)
            with act.Fori(0, B) as b:
                for t in range(ST):
                    act.wait_ge(tr_done, b * 4 + t + 1)
                    act.activation(xT_hi[:, :, t * P:(t + 1) * P], h_ps[t % 2][:].rearrange("p a (k t) -> p (a k) t", t=P),
                                   ACT.Copy).then_inc(xt_hi, 1)
                with act.Fori(0, STEPS) as j:
                    n = b * STEPS + j
                    act.wait_ge(w1_loaded, n * 16 + 16)
                    act.wait_ge(up_done, n * FT + 1)
                    act.activation(w1_hi[:].rearrange("p k n -> p (k n)"), w_raw[:, 0, :], ACT.Copy).then_inc(w1_hi_ready, 1)
                    act.wait_ge(w2_loaded, n * 16 + 16)
                    act.wait_ge(down_done, n * ST + 1)
                    act.activation(w2_hi[:].rearrange("p k n -> p (k n)"), w_raw[:, 1, :], ACT.Copy).then_inc(w2_hi_ready, 1)
                    for f in range(FT):
                        act.wait_ge(up_done, n * FT + f + 1 + 1)
                        if f < 2:
                            act.wait_ge(h_lo_ready, n * FT + 1)
                        else:
                            act.wait_ge(h_lo_ready, n * FT + f - 1 + 1)
                        act.activation(h[:, f % 2, :], h_ps[f // 2][:, f % 2, :], ACT.Gelu_apprx_tanh,
                                       bias=b1[:, ds(j * FT + f, 1)]).then_inc(h_ready, 1)
                        act.wait_ge(h_ready, n * FT + f + 1)
                        act.activation(h_hi[:, f, :], h[:, f % 2, :], ACT.Copy).then_inc(h_hi_ready, 1)

        @block.vector
        def _(dve):
            dve.sem_inc(h_lo_ready, 1)
            dve.sem_inc(added, 1)
            dve.sem_inc(xn_ready, 1)
            dve.wait_ge(const_in, 48)
            with dve.Fori(0, B) as b:
                dve.wait_ge(x_loaded, b * 16 + 16)
                for t in range(ST):
                    first = (b * 4 + t) * 3
                    for hh in range(2):
                        dve.bn_stats(stats[:, hh, :], x2[:, t, hh * HALF:(hh + 1) * HALF]).then_inc(step, 1)
                    dve.wait_ge(xn_ready, b * 4 + t + 1)
                    hold(dve, step, first + 2, held["dve"])
                    dve.bn_aggr(mv[:], stats[:]).then_inc(step, 1)
                    dve.wait_ge(step, first + 3)
                    dve.tensor_scalar(var_eps[:], mv[:, 1:2], LN_EPS, None, ALU.add).then_inc(var_ready, 1)
                    dve.wait_ge(rstd_ready, b * 4 + t + 1)
                    if t >= 2:
                        dve.wait_ge(tr_done, b * 4 + t - 1)
                    dve.tensor_scalar(xn[:, t % 2, :], x2[:, t, 0:C], mv[:, 0:1], rstd[:, 0:1], ALU.subtract,
                                      ALU.mult).then_inc(xn_ready, 1)
                    dve.wait_ge(rows_left, b + 1)
                    dve.tensor_tensor(acc[:, t, :], x2[:, t, 0:C], b2[:], ALU.add).then_inc(acc_set, 1)
                    dve.wait_ge(xt_hi, b * 4 + t + 1)
                    dve.tensor_tensor(xT_lo[:, :, t * P:(t + 1) * P], h_ps[t % 2][:].rearrange("p a (k t) -> p (a k) t", t=P),
                                      xT_hi[:, :, t * P:(t + 1) * P].bitcast(F32), ALU.subtract).then_inc(xt_lo, 1)
                with dve.Fori(0, STEPS) as j:
                    n = b * STEPS + j
                    for f in range(FT):
                        dve.wait_ge(h_hi_ready, n * FT + f + 1)
                        dve.tensor_tensor(h_lo[:, f, :], h[:, f % 2, :], h_hi[:, f, :].bitcast(F32), ALU.subtract).then_inc(h_lo_ready, 1)
                    dve.wait_ge(acc_set, b * 4 + 4)
                    dve.wait_ge(added, n * ST + 1)
                    for t in range(ST):
                        dve.wait_ge(down_done, n * ST + t + 1 + 1)
                        dve.tensor_tensor(acc[:, t, :], o_ps[t % 2][:].rearrange("p a n -> p (a n)"), acc[:, t, :], ALU.add).then_inc(added, 1)
                dve.wait_ge(added, b * STEPS * ST + STEPS * ST + 1)
                dve.sem_inc(final_ready, 4)

        @block.tensor
        def _(pe):
            pe.sem_inc(up_done, 1)
            pe.sem_inc(down_done, 1)
            pe.wait_ge(const_in, 48)
            with pe.Fori(0, B) as b:
                for t in range(ST):
                    pe.wait_ge(xn_ready, b * 4 + t + 1 + 1)
                    if t >= 2:
                        pe.wait_ge(xt_lo, b * 4 + t - 1)
                    for k in range(KT):
                        mm = pe.transpose(h_ps[t % 2][:, k // 4, k % 4 * P:k % 4 * P + P], xn[:, t % 2, k * P:(k + 1) * P], ident[:])
                    mm.then_inc(tr_done, 1)
                hold(pe, xt_lo, b * 4 + 4, held["pe"])
                with pe.Fori(0, STEPS) as j:
                    n = b * STEPS + j
                    pe.wait_ge(w1_lo_ready, n + 1 + 1)
                    for f in range(FT):
                        for k in range(KT):
                            mm = product3(pe, h_ps[f // 2][:, f % 2, :], w1_hi[:, k, f * P:(f + 1) * P], w1_lo[:, k, f * P:(f + 1) * P],
                                          xT_hi[:, k, :], xT_lo[:, k, :], k == 0, k == KT - 1)
                        mm.then_inc(up_done, 1)
                    pe.wait_ge(w2_lo_ready, n + 1 + 1)
                    for t in range(ST):
                        if t < 2:
                            pe.wait_ge(added, n * ST + 1)
                        else:
                            pe.wait_ge(added, n * ST + t - 1 + 1)
                        for c in range(2):
                            for f in range(FT):
                                if t == 0 and c == 0:
                                    pe.wait_ge(h_lo_ready, n * FT + f + 1 + 1)
                                mm = product3(pe, o_ps[t % 2][:, c, :], h_hi[:, f, t * P:(t + 1) * P], h_lo[:, f, t * P:(t + 1) * P],
                                              w2_hi[:, f, c * HALF:(c + 1) * HALF], w2_lo[:, f, c * HALF:(c + 1) * HALF],
                                              f == 0, f == FT - 1)
                        mm.then_inc(down_done, 1)


def build(nc, x, ctxT, w_kvq, w_p, b_p, w_decay, u_bonus, w_r, b_r, w1, b1, w2, b2, head_mask, identity, earlier, token, out):
    x1_dram = nc.dram_tensor("x1", [B * T, C], F32).ap()
    kT_dram = nc.dram_tensor("kT", [B * C, T], F32).ap()
    y_dram = nc.dram_tensor("y", [B * T, C], F32).ap()
    score_dram = nc.dram_tensor("score", [B * T], F32).ap()
    sel_dram = nc.dram_tensor("sel", [B * T, C + 1], F32).ap()
    attention_phase(nc, x, w_kvq, w_p, b_p, head_mask, identity, x1_dram, kT_dram)
    wkv_phase(nc, kT_dram, ctxT, w_decay, u_bonus, identity, y_dram)
    select_phase(nc, x1_dram, y_dram, w_r, b_r, earlier, token, score_dram, sel_dram, out)
    ffn_phase(nc, sel_dram, w1, b1, w2, b2, identity, out)


def kernel(x, ctx_2048, L0_attn_w_qkv, L0_attn_w_proj, L0_attn_b_proj, L0_xattn_w, L0_xattn_u, L0_ffn_w_r, L0_ffn_b_r,
           L0_ffn_w1, L0_ffn_b1, L0_ffn_w2, L0_ffn_b2):
    import numpy as np
    import concourse.bacc as bacc
    from concourse.bass_utils import run_bass_kernel_spmd

    def tiled(w, cols):
        k, n = w.shape[0] // P, w.shape[1] // cols
        return w.reshape(k, P, n, cols).transpose(2, 1, 0, 3).reshape(n * P, k * cols)

    def columns(v):
        return v.reshape(-1, P).T

    w_q, w_k, w_v = (np.asarray(L0_attn_w_qkv)[i * C:(i + 1) * C].T for i in range(3))
    w_kv = np.stack([w_k.reshape(C, KT, P), w_v.reshape(C, KT, P)], axis=2).reshape(C, 2 * C)
    part, col = np.arange(P)[:, None], np.arange(T)[None, :]
    token = part + P * np.arange(TT)[None, :]
    arrays = {
        "x": np.asarray(x).reshape(B * T, C),
        "ctxT": np.asarray(ctx_2048).transpose(0, 2, 1).reshape(B * C, T),
        "w_kvq": np.concatenate([tiled(w_kv, 256), tiled(w_q, 256)]),
        "w_p": tiled(np.asarray(L0_attn_w_proj).T, 256),
        "b_p": np.asarray(L0_attn_b_proj),
        "w_decay": columns(np.asarray(L0_xattn_w)),
        "u_bonus": columns(np.asarray(L0_xattn_u)),
        "w_r": np.asarray(L0_ffn_w_r),
        "b_r": np.asarray(L0_ffn_b_r).reshape(1),
        "w1": tiled(np.asarray(L0_ffn_w1), CHUNK),
        "b1": columns(np.asarray(L0_ffn_b1)),
        "w2": np.asarray(L0_ffn_w2),
        "b2": np.asarray(L0_ffn_b2),
        "head_mask": (part // HEAD == col[:, :P] // HEAD).astype(np.float32),
        "identity": np.eye(P, dtype=np.float32),
        "earlier": (token.reshape(1, 1, T) < token[:, :, None]).astype(np.float32).reshape(P, TT * T),
        "token": token.astype(np.float32),
    }
    nc = bacc.Bacc("TRN2", target_bir_lowering=False, num_devices=1)
    args = []
    for name, a in arrays.items():
        arrays[name] = a = np.ascontiguousarray(a)
        args.append(nc.dram_tensor(name, a.shape, mybir.dt.from_np(a.dtype), kind="ExternalInput").ap())
    args.append(nc.dram_tensor("out", (B * T, C), F32, kind="ExternalOutput").ap())
    build(nc, *args)
    r = run_bass_kernel_spmd(nc, [arrays], core_ids=[0])
    return r.results[0]["out"].reshape(B, T, C)
```

```python
from contextlib import ExitStack

import concourse.bass as bass
from concourse import mybir

F32 = mybir.dt.float32
F32R = mybir.dt.float32r
I32 = mybir.dt.int32
ACT = mybir.ActivationFunctionType
ALU = mybir.AluOpType
ds = bass.ds

P = 128
B, T, C = 4, 1024, 1024
KT = C // P
TT = T // P
HALF = 512
HEAD = 32
DF = 4 * C
SEL = T // 2
CHUNK = 256
FT = CHUNK // P
STEPS = DF // CHUNK
ST = SEL // P
UNITS = 2 * KT
LN_EPS = 1e-5
ATT_EPS = 1e-15
NO_PAST = -1e38
R_CLAMP = 40.0
JUST_BELOW_0 = -1.2e-38


class Tools:

    def __init__(self, nc, ctx, tag):
        self.nc, self.ctx, self.tag = nc, ctx, tag

    def sb(self, name, shape, dt=F32):
        return self.ctx.enter_context(self.nc.sbuf_tensor(f"{self.tag}_{name}", shape, dt))

    def ps(self, name, shape):
        return self.ctx.enter_context(self.nc.psum_tensor(f"{self.tag}_{name}", shape, F32))

    def sem(self, name):
        return self.ctx.enter_context(self.nc.semaphore(f"{self.tag}_{name}"))


def hold(engine, sem, value, spare):
    engine.wait_ge(sem, value)
    engine.sem_inc(spare, 1)


def product3(pe, out, w_hi, w_lo, x_hi, x_lo, start, stop):
    pe.matmul(out, w_hi, x_hi, start=start, stop=False)
    pe.matmul(out, w_hi, x_lo, start=False, stop=False)
    return pe.matmul(out, w_lo, x_hi, start=False, stop=stop)


def attention_phase(nc, x, w_kvq, w_p, b_p, consts_mask, ident_in, x1_dram, kT_dram):
    with ExitStack() as ctx:
        m = Tools(nc, ctx, "att")
        x_tok = m.sb("x_tok", [P, 2, C])
        xn = m.sb("xn", [P, 2, C])
        act_hi = m.sb("act_hi", [P, KT, T], F32R)
        act_lo = m.sb("act_lo", [P, KT, T], F32R)
        w_raw = m.sb("w_raw", [P, 2, 2048])
        w_hi = m.sb("w_hi", [P, 2, 2048], F32R)
        w_lo = m.sb("w_lo", [P, 2, 2048], F32R)
        kvb_hi = m.sb("kvb_hi", [P, KT, 256], F32R)
        kvb_lo = m.sb("kvb_lo", [P, KT, 256], F32R)
        kvb = m.sb("kvb", [P, 256])
        kT = m.sb("kT", [P, 2, KT, P])
        bias = m.sb("bias", [P, C])
        mask = m.sb("mask", [P, P])
        ident = m.sb("ident", [P, P])
        stats = m.sb("stats", [P, 2, 6])
        mv = m.sb("mv", [P, 2])
        var_eps = m.sb("var_eps", [P, 1])
        minus_half = m.sb("minus_half", [P, 1])
        rstd = m.sb("rstd", [P, 1])
        with ExitStack() as kv_only:
            k = Tools(nc, kv_only, "attk")
            kv_hi = k.sb("kv_hi", [P, TT, 258], F32R)
            kv_lo = k.sb("kv_lo", [P, TT, 258], F32R)
        q_hi = m.sb("q_hi", [P, 2, HALF], F32R)
        q_lo = m.sb("q_lo", [P, 2, HALF], F32R)
        rden = m.sb("rden", [P, HALF])
        o = m.sb("o", [P, KT, T])
        pair = [m.ps(f"pair{i}", [P, 2, HALF]) for i in range(4)]

        const_in = m.sem("const_in")
        x_loaded = [m.sem(f"x_loaded{s}") for s in range(2)]
        stat_step, var_ready, rstd_ready = m.sem("stat_step"), m.sem("var_ready"), m.sem("rstd_ready")
        half_set = m.sem("half_set")
        xn_ready, tr_done = m.sem("xn_ready"), m.sem("tr_done")
        xt_hi, xt_lo = m.sem("xt_hi"), m.sem("xt_lo")
        raw_loaded = [m.sem(f"raw_loaded{s}") for s in range(2)]
        w_hi_ready, w_lo_ready = m.sem("w_hi_ready"), m.sem("w_lo_ready")
        kv_main, kv_hi_ready, kv_lo_ready = m.sem("kv_main"), m.sem("kv_hi_ready"), m.sem("kv_lo_ready")
        kv_free, vk_done = m.sem("kv_free"), m.sem("vk_done")
        ones_set = m.sem("ones_set")
        kvb_hi_ready, kvb_lo_ready = m.sem("kvb_hi_ready"), m.sem("kvb_lo_ready")
        kvb_made = m.sem("kvb_made")
        q_main, q_hi_ready, q_lo_ready = m.sem("q_main"), m.sem("q_hi_ready"), m.sem("q_lo_ready")
        nd_done, o_done, rden_step = m.sem("nd_done"), m.sem("o_done"), m.sem("rden_step")
        wp_lo_dve = m.sem("wp_lo_dve")
        os_hi_ready, os_lo_ready = m.sem("os_hi_ready"), m.sem("os_lo_ready")
        xb_ready, proj_done, x1_ready = m.sem("xb_ready"), m.sem("proj_done"), m.sem("x1_ready")
        x1_stored = [m.sem(f"x1_stored{s}") for s in range(2)]
        kt_evac = m.sem("kt_evac")
        kt_stored = [m.sem(f"kt_stored{s}") for s in range(2)]
        held = {e: m.sem(f"held_{e}") for e in ("sp", "act", "pool", "pe", "dve")}
        block = ctx.enter_context(nc.Block())

        def w_view(w, s):
            return w[:, s, :].rearrange("p (k n) -> p k n", k=KT)

        def o_view(w, s):
            return w[:, s, 0:KT * P].rearrange("p (k n) -> p k n", k=KT)

        @block.sync
        def _(sp):
            sp.dma_start(mask[:], consts_mask).then_inc(const_in, 16)
            sp.dma_start(ident[:], ident_in).then_inc(const_in, 16)
            sp.dma_start(bias[:], b_p.rearrange("(a n) -> a n", a=1).to_broadcast([P, C])).then_inc(const_in, 16)

            def load_weights(b, idx, s, src, row):
                sp.wait_ge(w_lo_ready, b * 16 + idx + 1)
                sp.dma_start(w_raw[:, s, :], src[ds(row * P, P), :]).then_inc(raw_loaded[s], 16)

            def load_x(b, n, t, s):
                sp.wait_ge(xn_ready, b * 16 + n + 1)
                sp.dma_start(x_tok[:, s, :], x[ds(b * T + t * P, P), :]).then_inc(x_loaded[s], 16)

            def store_x1(b, t, s):
                sp.wait_ge(x1_ready, b * 8 + t + 1 + 2)
                sp.dma_start(x1_dram[ds(b * T + t * P, P), :], x_tok[:, s, :]).then_inc(x1_stored[s], 16)

            with sp.Fori(0, B) as b:
                for s in range(2):
                    load_x(b, s, s, s)
                    load_weights(b, s, s, w_kvq, s)
                with sp.Fori(1, TT // 2) as i:
                    for s in range(2):
                        load_x(b, i * 2 + s, i * 2 + s, s)
                for s in range(2):
                    load_x(b, 8 + s, s, s)
                with sp.Fori(1, 6) as i:
                    for s in range(2):
                        load_weights(b, i * 2 + s, s, w_kvq, i * 2 + s)
                with sp.Fori(0, 2) as i:
                    for s in range(2):
                        load_weights(b, i * 2 + s + 12, s, w_p, i * 2 + s)
                with sp.Fori(0, TT // 2 - 1) as i:
                    for s in range(2):
                        store_x1(b, i * 2 + s, s)
                        hold(sp, x1_stored[s], b * 64 + i * 16 + 16, held["sp"])
                        load_x(b, i * 2 + s + 10, i * 2 + s + 2, s)
                for s in range(2):
                    store_x1(b, TT - 2 + s, s)
                for s in range(2):
                    hold(sp, x1_stored[s], b * 64 + 64, held["sp"])

        def layer_norm(dve, src, dst, n):
            for h in range(2):
                dve.bn_stats(stats[:, h, :], src[:, h * HALF:(h + 1) * HALF]).then_inc(stat_step, 1)
            dve.wait_ge(xn_ready, n + 2)
            hold(dve, stat_step, n * 3 + 2, held["dve"])
            dve.bn_aggr(mv[:], stats[:]).then_inc(stat_step, 1)
            dve.wait_ge(stat_step, n * 3 + 3)
            dve.tensor_scalar(var_eps[:], mv[:, 1:2], LN_EPS, None, ALU.add).then_inc(var_ready, 1)
            dve.wait_ge(rstd_ready, n + 1)
            return dve.tensor_scalar(dst, src, mv[:, 0:1], rstd[:, 0:1], ALU.subtract, ALU.mult)

        @block.vector
        def _(dve):
            dve.sem_inc(xn_ready, 2)
            dve.sem_inc(xt_lo, 2)
            dve.sem_inc(kv_lo_ready, 4)
            dve.sem_inc(kvb_made, 4)
            dve.sem_inc(q_lo_ready, 4)
            dve.sem_inc(o_done, 2)
            dve.sem_inc(x1_ready, 2)
            dve.sem_inc(kvb_lo_ready, 1)
            dve.wait_ge(const_in, 48)
            with dve.Fori(0, B) as b:
                def norm(t):
                    s = t % 2
                    dve.wait_ge(x_loaded[s], b * 128 + t // 2 * 16 + 16)
                    dve.wait_ge(tr_done, b * 16 + t + 1)
                    layer_norm(dve, x_tok[:, s, :], xn[:, s, :], b * 16 + t).then_inc(xn_ready, 1)

                def low_xt(t):
                    dve.wait_ge(xt_hi, b * 8 + t + 1)
                    dve.tensor_tensor(act_lo[:, :, t * P:(t + 1) * P], pair[3][:].rearrange("p a (k t) -> p (a k) t", t=P),
                                      act_hi[:, :, t * P:(t + 1) * P].bitcast(F32), ALU.subtract).then_inc(xt_lo, 1)

                def low_kv(g, t):
                    bank = pair[t % 4 // 2][:, t % 2, :]
                    dve.wait_ge(kv_hi_ready, (b * 8 + g) * 8 + t + 1)
                    dve.scalar_tensor_tensor(kv_lo[:, t, 0:P], bank[:, 0:P], 0.0, kv_hi[:, t, 0:P].bitcast(F32),
                                             ALU.max, ALU.subtract)
                    dve.tensor_tensor(kv_lo[:, t, P:2 * P], bank[:, P:2 * P], kv_hi[:, t, P:2 * P].bitcast(F32),
                                      ALU.subtract).then_inc(kv_lo_ready, 1)

                def head_blocks(g, s):
                    vk = pair[2][:, s, :]
                    dve.wait_ge(kvb_lo_ready, b * 8 + g + 1)
                    dve.wait_ge(vk_done, b * 8 + g + 1 + 1)
                    dve.tensor_tensor(kvb[:, 0:P], vk[:, 0:P], mask[:], ALU.mult).then_inc(kvb_made, 1)
                    dve.tensor_scalar(kvb[:, P:2 * P], mask[:], vk[:, P:P + 1], None, ALU.mult).then_inc(kvb_made, 1)
                    dve.wait_ge(kvb_hi_ready, b * 8 + g + 1)
                    dve.tensor_tensor(kvb_lo[:, ds(g, 1), :].rearrange("p a n -> p (a n)"),
                                      kvb[:], kvb_hi[:, ds(g, 1), :].rearrange("p a n -> p (a n)").bitcast(F32),
                                      ALU.subtract).then_inc(kvb_lo_ready, 1)

                def group(g, s):
                    for t in range(TT):
                        low_kv(g, t)
                    head_blocks(g, s)

                norm(0)
                dve.wait_ge(o_done, b * 16 + 2)
                dve.memset(kv_hi[:, :, 256:258].bitcast(F32), 1.0).then_inc(ones_set, 1)
                dve.memset(kv_lo[:, :, 256:258].bitcast(F32), 0.0).then_inc(ones_set, 1)
                for t in range(TT):
                    if t < TT - 1:
                        norm(t + 1)
                    low_xt(t)
                    if t:
                        low_kv(0, t - 1)
                low_kv(0, TT - 1)
                head_blocks(0, 0)
                with dve.Fori(0, KT // 2 - 1) as i:
                    group(i * 2 + 1, 1)
                    group(i * 2 + 2, 0)
                group(KT - 1, 1)

                def attend(u):
                    dve.wait_ge(o_done, b * 16 + u + 2)
                    dve.wait_ge(nd_done, b * 16 + u + 1 + 2)
                    dve.tensor_scalar(rden[:], pair[2 + u % 2][:, 1, :], ATT_EPS, None, ALU.add).then_inc(rden_step, 1)
                    dve.wait_ge(rden_step, (b * 16 + u) * 2 + 1)
                    dve.reciprocal(rden[:], rden[:]).then_inc(rden_step, 1)
                    dve.wait_ge(rden_step, (b * 16 + u) * 2 + 2)
                    dve.tensor_tensor(o[:, u // 2, u % 2 * HALF:u % 2 * HALF + HALF], pair[2 + u % 2][:, 0, :], rden[:],
                                      ALU.mult).then_inc(o_done, 1)

                for u in range(16):
                    dve.wait_ge(q_hi_ready, b * 16 + u + 1)
                    dve.scalar_tensor_tensor(q_lo[:, u % 2, :], pair[u % 4 // 2][:, u % 2, :], 0.0,
                                             q_hi[:, u % 2, :].bitcast(F32), ALU.max, ALU.subtract).then_inc(q_lo_ready, 1)
                    if u:
                        attend(u - 1)
                attend(15)
                for j in (1, 3):
                    dve.wait_ge(w_hi_ready, b * 16 + 12 + j + 1)
                    cols = slice(j * 256, j * 256 + 256)
                    dve.tensor_tensor(act_lo[:, :, cols], w_view(w_raw, j % 2), act_hi[:, :, cols].bitcast(F32),
                                      ALU.subtract).then_inc(wp_lo_dve, 1)

                def low_o(t):
                    s = t % 2
                    dve.wait_ge(os_hi_ready, b * 8 + t + 1)
                    dve.tensor_tensor(o_view(w_lo, s), o[:, :, t * P:(t + 1) * P], o_view(w_hi, s).bitcast(F32),
                                      ALU.subtract).then_inc(os_lo_ready, 1)

                low_o(0)
                for t in range(TT):
                    s = t % 2
                    if t < TT - 1:
                        low_o(t + 1)
                    dve.wait_ge(proj_done, b * 8 + t + 1 + 2)
                    dve.wait_ge(xb_ready, b * 8 + t + 1)
                    dve.tensor_tensor(x_tok[:, s, :], pair[s][:].rearrange("p a n -> p (a n)"), x_tok[:, s, :],
                                      ALU.add).then_inc(x1_ready, 1)
                    dve.wait_ge(x1_ready, b * 8 + t + 1 + 2)
                    dve.wait_ge(tr_done, b * 16 + 8 + t + 1)
                    layer_norm(dve, x_tok[:, s, :], xn[:, s, :], b * 16 + 8 + t).then_inc(xn_ready, 1)

        @block.gpsimd
        def _(pool):
            pool.sem_inc(w_lo_ready, 2)
            pool.memset(minus_half[:], -0.5).then_inc(half_set, 1)
            pool.wait_ge(half_set, 1)
            pool.wait_ge(const_in, 48)

            def low_weights(b, i, s):
                pool.wait_ge(w_hi_ready, b * 16 + i * 2 + s + 1)
                pool.tensor_tensor(w_lo[:, s, :], w_raw[:, s, :], w_hi[:, s, :].bitcast(F32),
                                   ALU.subtract).then_inc(w_lo_ready, 1)

            def inverse_deviation(n):
                pool.wait_ge(var_ready, n + 1)
                pool.tensor_tensor(rstd[:], var_eps[:], minus_half[:], ALU.pow).then_inc(rstd_ready, 1)

            with pool.Fori(0, B) as b:
                for s in range(2):
                    low_weights(b, 0, s)
                with pool.Fori(0, TT) as t:
                    inverse_deviation(b * 16 + t)
                with pool.Fori(1, 6) as i:
                    for s in range(2):
                        low_weights(b, i, s)
                for j in range(4):
                    pool.wait_ge(w_hi_ready, b * 16 + 12 + j + 1)
                    cols = slice(j * 256, j * 256 + 256)
                    if j % 2 == 0:
                        pool.tensor_tensor(act_lo[:, :, cols], w_view(w_raw, j % 2), act_hi[:, :, cols].bitcast(F32),
                                           ALU.subtract).then_inc(w_lo_ready, 1)
                    else:
                        pool.wait_ge(w_lo_ready, b * 16 + 12 + j + 2)
                        pool.wait_ge(wp_lo_dve, b * 2 + j // 2 + 1)
                        pool.sem_inc(w_lo_ready, 1)
                for t in range(TT):
                    s = t % 2
                    pool.wait_ge(x_loaded[s], b * 128 + 64 + t // 2 * 16 + 16)
                    pool.tensor_tensor(x_tok[:, s, :], x_tok[:, s, :], bias[:], ALU.add).then_inc(xb_ready, 1)
                    inverse_deviation(b * 16 + 8 + t)

        @block.scalar
        def _(act):
            act.sem_inc(kt_evac, 2)
            for s in range(2):
                act.sem_inc(kt_stored[s], 16)

            def high_weights(b, i, s):
                act.wait_ge(raw_loaded[s], b * 128 + i * 16 + 16)
                act.activation(w_hi[:, s, :], w_raw[:, s, :], ACT.Copy).then_inc(w_hi_ready, 1)

            with act.Fori(0, B) as b:
                act.wait_ge(proj_done, b * 8 + 2)
                for s in range(2):
                    high_weights(b, 0, s)
                def high_xt(t):
                    act.wait_ge(tr_done, b * 16 + t + 1 + 2)
                    act.activation(act_hi[:, :, t * P:(t + 1) * P], pair[3][:].rearrange("p a (k t) -> p (a k) t", t=P),
                                   ACT.Copy).then_inc(xt_hi, 1)

                def high_kv(g, t):
                    bank = pair[t % 4 // 2][:, t % 2, :]
                    act.wait_ge(kv_main, (b * 8 + g) * 8 + t + 1)
                    if t < TT - 1:
                        act.wait_ge(kv_free, (b * 8 + g) * 7 + t + 1)
                    else:
                        act.wait_ge(vk_done, b * 8 + g + 1)
                    act.activation(kv_hi[:, t, 0:P], bank[:, 0:P], ACT.Relu)
                    act.activation(kv_hi[:, t, P:2 * P], bank[:, P:2 * P], ACT.Copy).then_inc(kv_hi_ready, 1)

                def head_blocks_high(g):
                    act.wait_ge(kvb_made, (b * 8 + g) * 2 + 2 + 4)
                    act.activation(kvb_hi[:, ds(g, 1), :].rearrange("p a n -> p (a n)"), kvb[:],
                                   ACT.Copy).then_inc(kvb_hi_ready, 1)

                def group(g, s, i):
                    for t in range(TT):
                        high_kv(g, t)
                    head_blocks_high(g)
                    high_weights(b, i, s)

                for t in range(TT):
                    high_xt(t)
                    if t:
                        high_kv(0, t - 1)
                high_kv(0, TT - 1)
                head_blocks_high(0)
                high_weights(b, 1, 0)
                with act.Fori(0, KT // 2 - 1) as i:
                    group(i * 2 + 1, 1, i + 1)
                    group(i * 2 + 2, 0, i + 2)
                group(KT - 1, 1, KT // 2)
                for u in range(16):
                    act.wait_ge(q_main, b * 16 + u + 1)
                    act.wait_ge(nd_done, b * 16 + u + 1)
                    act.activation(q_hi[:, u % 2, :], pair[u % 4 // 2][:, u % 2, :], ACT.Relu).then_inc(q_hi_ready, 1)
                    if u in (4, 8):
                        high_weights(b, 5, u // 4 - 1)
                with act.Fori(0, 2) as i:
                    for s in range(2):
                        act.wait_ge(raw_loaded[s], b * 128 + 96 + i * 16 + 16)
                        act.activation(act_hi[:, :, ds((i * 2 + s) * 256, 256)], w_view(w_raw, s),
                                       ACT.Copy).then_inc(w_hi_ready, 1)

                def high_o(t):
                    s = t % 2
                    act.wait_ge(o_done, b * 16 + (15 if t < TT // 2 else 16) + 2)
                    act.wait_ge(proj_done, b * 8 + t + 1)
                    act.activation(o_view(w_hi, s), o[:, :, t * P:(t + 1) * P], ACT.Copy).then_inc(os_hi_ready, 1)

                def turned_k(t):
                    s = t % 2
                    act.wait_ge(tr_done, b * 16 + 8 + t + 1 + 2)
                    act.wait_ge(kt_stored[s], b * 64 + t // 2 * 16 + 16)
                    act.activation(kT[:, s, :, :], pair[2 + s][:].rearrange("p a (k t) -> p (a k) t", t=P),
                                   ACT.Copy).then_inc(kt_evac, 1)
                    act.wait_ge(kt_evac, b * 8 + t + 1 + 2)
                    act.dma_start(kT_dram[ds(b * C, C), t * P:(t + 1) * P].rearrange("(k c) t -> c k t", c=P),
                                  kT[:, s, :, :]).then_inc(kt_stored[s], 16)

                high_o(0)
                high_o(1)
                for t in range(TT):
                    if t:
                        turned_k(t - 1)
                    if t + 2 < TT:
                        high_o(t + 2)
                turned_k(TT - 1)
            for s in range(2):
                act.wait_ge(kt_stored[s], B * 64 + 16)

        @block.tensor
        def _(pe):
            pe.sem_inc(tr_done, 2)
            pe.sem_inc(kv_free, TT - 1)
            pe.sem_inc(nd_done, 2)
            pe.sem_inc(proj_done, 2)
            pe.sem_inc(vk_done, 1)
            pe.wait_ge(const_in, 48)
            with pe.Fori(0, B) as b:
                def turn_xn(t):
                    pe.wait_ge(xn_ready, b * 16 + t + 1 + 2)
                    pe.wait_ge(xt_lo, b * 8 + t + 2)
                    for k in range(KT):
                        mm = pe.transpose(pair[3][:, k // 4, k % 4 * P:k % 4 * P + P],
                                          xn[:, t % 2, k * P:(k + 1) * P], ident[:])
                    mm.then_inc(tr_done, 1)

                def k_and_v(g, s, t):
                    pe.wait_ge(kv_lo_ready, (b * 8 + g) * 8 + t + 1)
                    for k in range(KT):
                        mm = product3(pe, pair[t % 4 // 2][:, t % 2, 0:256],
                                      act_hi[:, k, t * P:(t + 1) * P], act_lo[:, k, t * P:(t + 1) * P],
                                      w_view(w_hi, s)[:, k, :], w_view(w_lo, s)[:, k, :], k == 0, k == KT - 1)
                    mm.then_inc(kv_main, 1)

                def k_times_v(g, s, t):
                    pe.wait_ge(kv_lo_ready, (b * 8 + g) * 8 + t + 1 + 4)
                    mm = product3(pe, pair[2][:, s, 0:130], kv_hi[:, t, 0:P], kv_lo[:, t, 0:P],
                                  kv_hi[:, t, P:258], kv_lo[:, t, P:258], t == 0, t == TT - 1)
                    mm.then_inc(vk_done if t == TT - 1 else kv_free, 1)

                def group_start(g):
                    pe.wait_ge(w_lo_ready, b * 16 + g + 1 + 2)
                    pe.wait_ge(kvb_made, (b * 8 + g) * 2 + 2)

                def group(g, s):
                    group_start(g)
                    for t in range(TT):
                        k_and_v(g, s, t)
                        if t:
                            k_times_v(g, s, t - 1)
                    k_times_v(g, s, TT - 1)

                pe.wait_ge(kt_evac, b * 8 + 2)
                turn_xn(0)
                group_start(0)
                pe.wait_ge(ones_set, b * 2 + 2)
                for t in range(TT):
                    if t < TT - 1:
                        turn_xn(t + 1)
                    pe.wait_ge(xt_lo, b * 8 + t + 1 + 2)
                    k_and_v(0, 0, t)
                    if t:
                        k_times_v(0, 0, t - 1)
                k_times_v(0, 0, TT - 1)
                with pe.Fori(0, KT // 2 - 1) as i:
                    group(i * 2 + 1, 1)
                    group(i * 2 + 2, 0)
                group(KT - 1, 1)

                def numerator_denominator(u):
                    c = u // 2
                    pe.wait_ge(q_lo_ready, b * 16 + u + 1 + 4)
                    pe.wait_ge(o_done, b * 16 + u + 1)
                    for h in range(2):
                        mm = product3(pe, pair[2 + u % 2][:, h, :], kvb_hi[:, c, h * P:(h + 1) * P], kvb_lo[:, c, h * P:(h + 1) * P],
                                      q_hi[:, u % 2, :], q_lo[:, u % 2, :], True, True)
                    mm.then_inc(nd_done, 1)

                for u in range(16):
                    c, h = u // 2, u % 2
                    s = c // 2 % 2
                    if u % 4 == 0:
                        pe.wait_ge(w_lo_ready, b * 16 + 8 + c // 2 + 1 + 2)
                    pe.wait_ge(q_lo_ready, b * 16 + u + 1)
                    for k in range(KT):
                        mm = product3(pe, pair[u % 4 // 2][:, u % 2, :],
                                      w_view(w_hi, s)[:, k, c % 2 * P:c % 2 * P + P], w_view(w_lo, s)[:, k, c % 2 * P:c % 2 * P + P],
                                      act_hi[:, k, h * HALF:(h + 1) * HALF], act_lo[:, k, h * HALF:(h + 1) * HALF],
                                      k == 0, k == KT - 1)
                    mm.then_inc(q_main, 1)
                    if u == 0:
                        pe.wait_ge(kvb_lo_ready, b * 8 + 8 + 1)
                    if u:
                        numerator_denominator(u - 1)
                numerator_denominator(15)

                def project(t):
                    s = t % 2
                    pe.wait_ge(os_lo_ready, b * 8 + t + 1)
                    pe.wait_ge(x1_ready, b * 8 + t + 1)
                    for h in range(2):
                        if t == 0:
                            pe.wait_ge(w_lo_ready, b * 16 + 14 + h * 2 + 2)
                        for k in range(KT):
                            mm = product3(pe, pair[s][:, h, :], o_view(w_hi, s)[:, k, :], o_view(w_lo, s)[:, k, :],
                                          act_hi[:, k, h * HALF:(h + 1) * HALF], act_lo[:, k, h * HALF:(h + 1) * HALF],
                                          k == 0, k == KT - 1)
                    mm.then_inc(proj_done, 1)

                def turn_k(t):
                    s = t % 2
                    pe.wait_ge(xn_ready, b * 16 + 8 + t + 1 + 2)
                    pe.wait_ge(kt_evac, b * 8 + t + 1)
                    for k in range(KT):
                        mm = pe.transpose(pair[2 + s][:, k // 4, k % 4 * P:k % 4 * P + P],
                                          xn[:, s, k * P:(k + 1) * P], ident[:])
                    mm.then_inc(tr_done, 1)

                for t in range(TT):
                    project(t)
                    if t:
                        turn_k(t - 1)
                turn_k(TT - 1)


def wkv_ffn_phase(nc, kT_dram, ctxT, x1_dram, w_in, u_in, wr_in, br_in, w1, b1_in, w2, b2_in, tie_in, tok_in, ident_in,
                  y_dram, x2_dram, score_dram, order_dram, out):
    with ExitStack() as ctx:
        m = Tools(nc, ctx, "mix")
        x2 = m.sb("x2", [P, ST, C])
        xn = m.sb("xn", [P, C])
        xT_hi = m.sb("xT_hi", [P, KT, SEL], F32R)
        xT_lo = m.sb("xT_lo", [P, KT, SEL], F32R)
        up_raw = m.sb("up_raw", [P, FT, KT * P])
        up_w_hi = m.sb("up_w_hi", [P, FT, KT * P], F32R)
        up_w_lo = m.sb("up_w_lo", [P, FT, KT * P], F32R)
        down_raw = m.sb("down_raw", [P, 2, FT * HALF])
        down_w_hi = m.sb("down_w_hi", [P, 2, FT * HALF], F32R)
        down_w_lo = m.sb("down_w_lo", [P, 2, FT * HALF], F32R)
        h = m.sb("h", [P, FT, SEL])
        h_hi = m.sb("h_hi", [P, 2, FT, SEL], F32R)
        h_lo = m.sb("h_lo", [P, 2, FT, SEL], F32R)
        acc = m.sb("acc", [P, ST, C])
        b1 = m.sb("b1", [P, DF // P])
        b2 = m.sb("b2", [P, C])
        ident = m.sb("ident", [P, P])
        stats = m.sb("stats", [P, ST, 2, 6])
        mv = m.sb("mv", [P, ST, 2])
        var_eps = m.sb("var_eps", [P, ST])
        minus_half = m.sb("minus_half", [P, ST])
        rstd = m.sb("rstd", [P, ST])
        chosen = m.sb("chosen", [P, ST], I32)
        mine = m.sb("mine", [P, ST], I32)
        first_row = m.sb("first_row", [P, 1])
        k = m.sb("k", [P, 2, HALF])
        v = m.sb("v", [P, 2, HALF])
        top = m.sb("top", [P, T + 1])
        p = m.sb("p", [P, T + 1])
        q = m.sb("q", [P, T + 1])
        decay = m.sb("decay", [P, 2, HALF])
        new = m.sb("new", [P, 2, HALF])
        own = m.sb("own", [P, 2, HALF])
        new_v = m.sb("new_v", [P, HALF])
        own_v = m.sb("own_v", [P, 2, HALF])
        guess = m.sb("guess", [P, HALF])
        better = m.sb("better", [P, HALF])
        y = m.sb("y", [P, 2, HALF])
        y_tok = m.sb("y_tok", [P, 2, HALF // P, P])
        w_col = m.sb("w_col", [P, KT])
        u_col = m.sb("u_col", [P, KT])
        w_now = m.sb("w_now", [P, 2])
        w_r = m.sb("w_r", [P, C])
        b_r = m.sb("b_r", [P, 1])
        tie = m.sb("tie", [P, T + TT])
        row_x = [a[:].rearrange("p a n -> p (a n)") for a in (new, own, decay, own_v)]
        row_y = [a[:].rearrange("p a n -> p (a n)") for a in (k, v)]
        all_scores = y_tok[:].rearrange("p a t n -> p (a t n)")
        scrap = y[:].rearrange("p a n -> p (a n)")
        tok = m.sb("tok", [P, TT])
        tok_i = m.sb("tok_i", [P, TT], I32)
        s_stats = m.sb("s_stats", [P, 2, 2, 6])
        s_mv = m.sb("s_mv", [P, 2, 2])
        s_var = m.sb("s_var", [P, 2])
        s_rstd = m.sb("s_rstd", [P, 2])
        product = m.sb("product", [P, TT])
        score = m.sb("score", [P, TT])
        rank = m.sb("rank", [P, TT])
        rank_i = m.sb("rank_i", [P, TT], I32)

        h_ps = m.ps("h_ps", [P, 2, HALF])
        o_ps = m.ps("o_ps", [P, 4, HALF])
        y_ps = m.ps("y_ps", [P, 2, HALF])

        const_in, half_set, start_set = m.sem("const_in"), m.sem("half_set"), m.sem("start_set")
        held = {e: m.sem(f"held_{e}") for e in ("sp", "act", "pool", "pe", "dve")}
        x2_in, ln_step, var_ready, rstd_ready = m.sem("x2_in"), m.sem("ln_step"), m.sem("var_ready"), m.sem("rstd_ready")
        xn_ready, tr_done, xt_hi, xt_lo = m.sem("xn_ready"), m.sem("tr_done"), m.sem("xt_hi"), m.sem("xt_lo")
        up_in = [m.sem(f"up_in{f}") for f in range(FT)]
        up_hi = [m.sem(f"up_hi{f}") for f in range(FT)]
        up_lo = [m.sem(f"up_lo{f}") for f in range(FT)]
        up_done = [m.sem(f"up_done{f}") for f in range(FT)]
        down_in = [m.sem(f"down_in{c}") for c in range(2)]
        down_hi = [m.sem(f"down_hi{c}") for c in range(2)]
        down_lo = [m.sem(f"down_lo{c}") for c in range(2)]
        down_done = [m.sem(f"down_done{c}") for c in range(2)]
        h_ready, h_hi_ready, h_lo_ready = m.sem("h_ready"), m.sem("h_hi_ready"), m.sem("h_lo_ready")
        added, acc_set, mine_set = m.sem("added"), m.sem("acc_set"), m.sem("mine_set")
        rows_stored, rows_left, chosen_in = m.sem("rows_stored"), m.sem("rows_left"), m.sem("chosen_in")
        k_in = [m.sem(f"k_in{s}") for s in range(2)]
        v_in = [m.sem(f"v_in{s}") for s in range(2)]
        column_ready, top_ready, clamped = m.sem("column_ready"), m.sem("top_ready"), m.sem("clamped")
        logs = m.sem("logs")
        exps = m.sem("exps")
        new_v_ready, own_v_ready = m.sem("new_v_ready"), m.sem("own_v_ready")
        state = m.sem("state")
        den_ready, num_ready = m.sem("den_ready"), m.sem("num_ready")
        guessed = m.sem("guessed")
        refined = m.sem("refined")
        y_ready, y_turned, y_evac = m.sem("y_ready"), m.sem("y_turned"), m.sem("y_evac")
        y_stored = [m.sem(f"y_stored{s}") for s in range(2)]
        row_x_in = [m.sem(f"row_x_in{s}") for s in range(4)]
        row_y_in = [m.sem(f"row_y_in{s}") for s in range(2)]
        row_ready, s_step = m.sem("row_ready"), m.sem("s_step")
        row_stored = [m.sem(f"row_stored{s}") for s in range(4)]
        s_var_ready, s_rstd_ready = m.sem("s_var_ready"), m.sem("s_rstd_ready")
        s_norm, s_product, score_ready = m.sem("s_norm"), m.sem("s_product"), m.sem("score_ready")
        score_stored, scores_in, ranked = m.sem("score_stored"), m.sem("scores_in"), m.sem("ranked")
        order_ready, first_row_set, order_stored = m.sem("order_ready"), m.sem("first_row_set"), m.sem("order_stored")
        block = ctx.enter_context(nc.Block())

        LOOPS, LOOP_STEPS, LOOP_UNITS = 2, 6, UNITS // 2
        REST = STEPS - LOOPS * LOOP_STEPS

        def half_of(place):
            return place // 4

        def head_place(t):
            return 2 * t + 2

        def turn_half(s):
            return half_of(5 * (s + 2)) + 1

        @block.sync
        def _(sp):
            def load_up(f, number, j):
                hold(sp, up_lo[f], number + 1, held["sp"])
                sp.dma_start(up_raw[:, f, :], w1[ds((j * FT + f) * P, P), :]).then_inc(up_in[f], 16)

            def load_down(c, number, j):
                hold(sp, down_lo[c], number + 1, held["sp"])
                sp.dma_start(down_raw[:, c, :].rearrange("p (f n) -> p f n", f=FT),
                             w2[ds(j * CHUNK, CHUNK), c * HALF:(c + 1) * HALF].rearrange("(f p) n -> p f n", p=P)).then_inc(down_in[c], 16)

            def load_k(U, row, s):
                hold(sp, logs, 3 * U + 1, held["sp"])
                sp.dma_start(k[:, s % 2, :], kT_dram[ds(row, P), s % 2 * HALF:(s % 2 + 1) * HALF]).then_inc(k_in[s % 2], 16)

            def load_v(U, row, s):
                hold(sp, own_v_ready, U + 1, held["sp"])
                hold(sp, new_v_ready, U + 1, held["sp"])
                sp.dma_start(v[:, s % 2, :], ctxT[ds(row, P), s % 2 * HALF:(s % 2 + 1) * HALF]).then_inc(v_in[s % 2], 16)

            def weave(b, ffn, nxt):
                a = b + 1
                if ffn:
                    for f in range(FT):
                        load_up(f, b * STEPS + 1, 1)
                if nxt and not (isinstance(a, int) and a == 0):
                    hold(sp, order_ready, a, held["sp"])
                    for r in range(4):
                        hold(sp, row_stored[r], a * 64, held["sp"])
                with sp.Fori(0, LOOPS) as i:
                    for jj in range(LOOP_STEPS):
                        j = i * LOOP_STEPS + jj
                        n = b * STEPS + j
                        if ffn:
                            load_down(1, n, j)
                        for half in range(2):
                            if ffn and half == 0:
                                load_up(0, n + 2, j + 2)
                                load_down(0, n + 1, j + 1)
                                load_up(1, n + 2, j + 2)
                            if nxt:
                                for s in range(LOOP_UNITS):
                                    U = a * UNITS + i * LOOP_UNITS + s
                                    row = (a * KT + i * (KT // 2) + s // 2) * P
                                    if half_of(max(0, 5 * (s - 1))) == 2 * jj + half:
                                        load_k(U, row, s)
                                    if half_of(5 * s) == 2 * jj + half:
                                        load_v(U, row, s)
                for jj in range(REST):
                    j = STEPS - REST + jj
                    n = b * STEPS + j
                    if ffn:
                        load_down(1, n, j)
                    for half in range(2):
                        if ffn and half == 0:
                            if j < STEPS - 1 and not (j == STEPS - 2 and not nxt):
                                load_up(0, n + 2, (j + 2) % STEPS)
                            if nxt or j < STEPS - 1:
                                load_down(0, n + 1, (j + 1) % STEPS)
                            if j < STEPS - 1 and not (j == STEPS - 2 and not nxt):
                                load_up(1, n + 2, (j + 2) % STEPS)
                        if nxt and jj == 0 and half == 0:
                            for s in range(2):
                                hold(sp, y_stored[s], (a + 1) * (UNITS // 2) * 16 + 16, held["sp"])
                        if nxt:
                            for t in range(TT):
                                if half_of(max(0, head_place(t - 1) if t else 0)) == 2 * jj + half:
                                    if t >= 4:
                                        hold(sp, row_stored[t % 4], a * 64 + 32, held["sp"])
                                    sp.dma_start(row_x[t % 4], x1_dram[ds(a * T, T), :].rearrange("(p t) c -> p t c", t=TT)[:, t, :]).then_inc(row_x_in[t % 4], 16)
                                    if t >= 2:
                                        hold(sp, s_product, a * TT + t - 1, held["sp"])
                                    sp.dma_start(row_y[t % 2].rearrange("p (i c) -> p i c", i=LOOPS),
                                                 y_dram[ds(a * LOOPS * T, LOOPS * T), :].rearrange("(i p t) c -> p t i c", i=LOOPS, t=TT)[:, t]).then_inc(row_y_in[t % 2], 16)
                    if nxt and jj == 2:
                        hold(sp, score_ready, a + 1, held["sp"])
                        sp.dma_start(score_dram[ds(a * T, T)].rearrange("(p t) -> p t", p=P), score[:]).then_inc(score_stored, 16)
                        hold(sp, score_stored, a * 16 + 16, held["sp"])
                        sp.dma_start(all_scores, score_dram[ds(a * T, T)].rearrange("(a n) -> a n", a=1).to_broadcast([P, T])).then_inc(scores_in, 16)
                if nxt:
                    hold(sp, order_stored, a * 128 + 128, held["sp"])
                    if ffn:
                        hold(sp, mine_set, b + 1, held["sp"])
                    sp.dma_start(chosen[:], order_dram[0:SEL, :].rearrange("(p t) a -> p (t a)", p=P)).then_inc(chosen_in, 16)

            sp.dma_start(ident[:], ident_in).then_inc(const_in, 16)
            sp.dma_start(w_col[:], w_in).then_inc(const_in, 16)
            sp.dma_start(u_col[:], u_in).then_inc(const_in, 16)
            sp.dma_start(tok[:], tok_in).then_inc(const_in, 16)
            sp.dma_start(b_r[:], br_in.rearrange("(a n) -> a n", a=1).to_broadcast([P, 1])).then_inc(const_in, 16)
            sp.dma_start(w_r[:], wr_in.rearrange("(a n) -> a n", a=1).to_broadcast([P, C])).then_inc(const_in, 16)
            sp.dma_start(tie[:], tie_in).then_inc(const_in, 16)
            sp.dma_start(b1[:], b1_in).then_inc(const_in, 16)
            sp.dma_start(b2[:], b2_in.rearrange("(a n) -> a n", a=1).to_broadcast([P, C])).then_inc(const_in, 16)
            load_up(0, 0, 0)
            load_up(1, 0, 0)
            load_down(0, 0, 0)
            weave(-1, False, True)
            with sp.Fori(0, B - 1) as b:
                weave(b, True, True)
            weave(B - 1, True, False)

        @block.gpsimd
        def _(pool):
            def split_up(f, number):
                pool.wait_ge(up_hi[f], number + 1)
                pool.tensor_tensor(up_w_lo[:, f, :], up_raw[:, f, :], up_w_hi[:, f, :].bitcast(F32), ALU.subtract).then_inc(up_lo[f], 1)

            def split_down(c, number):
                pool.wait_ge(down_hi[c], number + 1)
                pool.tensor_tensor(down_w_lo[:, c, :], down_raw[:, c, :], down_w_hi[:, c, :].bitcast(F32), ALU.subtract).then_inc(down_lo[c], 1)

            def unit_logs(U, s):
                lo = s % 2 * HALF
                pool.wait_ge(top_ready, U + 2)
                pool.wait_ge(refined, 2 * U + 1)
                pool.tensor_tensor(own[:, s % 2, :], k[:, s % 2, :], top[:, lo:lo + HALF], ALU.subtract).then_inc(logs, 1)
                pool.wait_ge(state, 2 * U + 1)
                pool.tensor_tensor(new[:, s % 2, :], k[:, s % 2, :], top[:, lo + 1:lo + HALF + 1], ALU.subtract).then_inc(logs, 1)
                pool.tensor_tensor(decay[:, s % 2, :], top[:, lo:lo + HALF], top[:, lo + 1:lo + HALF + 1], ALU.subtract).then_inc(logs, 1)

            def unit_own_v(U, s, loads):
                pool.wait_ge(exps, 3 * U + 3)
                pool.wait_ge(v_in[s % 2], loads)
                pool.wait_ge(y_ready, U + 1)
                pool.tensor_tensor(own_v[:, s % 2, :], own[:, s % 2, :], v[:, s % 2, :], ALU.mult).then_inc(own_v_ready, 1)

            def weave(b, ffn, nxt):
                a = b + 1
                if ffn:
                    if not (isinstance(b, int) and b == 0):
                        hold(pool, rows_stored, b * 64, held["pool"])
                    pool.sem_inc(rows_left, 1)
                    for f in range(FT):
                        split_up(f, b * STEPS + 1)
                with pool.Fori(0, LOOPS) as i:
                    for jj in range(LOOP_STEPS):
                        n = b * STEPS + i * LOOP_STEPS + jj
                        if ffn:
                            split_down(1, n)
                        for half in range(2):
                            if nxt:
                                for s in range(LOOP_UNITS + 1):
                                    if half_of(5 * s + 1) == 2 * jj + half:
                                        U = a * UNITS + i * LOOP_UNITS + s
                                        if s < LOOP_UNITS:
                                            unit_logs(U, s)
                                        if s >= 1:
                                            unit_own_v(U - 1, s - 1, (a * (UNITS // 2) + i * (LOOP_UNITS // 2) + (s - 1) // 2 + 1) * 16)
                            if ffn and half == 0:
                                split_up(0, n + 2)
                                split_down(0, n + 1)
                        if ffn:
                            split_up(1, n + 2)
                for jj in range(REST):
                    j = STEPS - REST + jj
                    n = b * STEPS + j
                    if ffn:
                        split_down(1, n)
                    for half in range(2):
                        if nxt:
                            for t in range(TT):
                                if half_of(head_place(t)) == 2 * jj + half:
                                    pool.wait_ge(s_var_ready, a * TT + t + 1)
                                    pool.tensor_tensor(s_rstd[:, t % 2:t % 2 + 1], s_var[:, t % 2:t % 2 + 1], minus_half[:, 0:1],
                                                       ALU.pow).then_inc(s_rstd_ready, 1)
                        if nxt and jj == REST - 1 and half == 0:
                            hold(pool, order_ready, a + 1, held["pool"])
                            for t in range(TT):
                                pool.indirect_dma_start(order_dram, bass.IndirectOffsetOnAxis(rank_i[:, t:t + 1], 0),
                                                        tok_i[:, t:t + 1], None).then_inc(order_stored, 16)
                        if nxt and jj == REST - 1 and half == 0:
                            hold(pool, chosen_in, a * 16 + 16, held["pool"])
                            for r in range(4):
                                hold(pool, row_stored[r], a * 64 + 64, held["pool"])
                            if ffn:
                                hold(pool, acc_set, b * ST + ST, held["pool"])
                            for t in range(ST):
                                pool.indirect_dma_start(x2[:, t, :], None, x2_dram, bass.IndirectOffsetOnAxis(chosen[:, t:t + 1], 0)).then_inc(x2_in, 16)
                        if ffn and half == 0:
                            if j < STEPS - 1 and not (j == STEPS - 2 and not nxt):
                                split_up(0, n + 2)
                            if nxt or j < STEPS - 1:
                                split_down(0, n + 1)
                    if ffn and j < STEPS - 1 and not (j == STEPS - 2 and not nxt):
                        split_up(1, n + 2)
                if nxt:
                    pool.wait_ge(var_ready, a * ST + ST)
                    pool.tensor_tensor(rstd[:], var_eps[:], minus_half[:], ALU.pow).then_inc(rstd_ready, 1)
                if ffn:
                    hold(pool, added, b * STEPS * 8 + STEPS * 8 + 4, held["pool"])
                    for t in range(ST):
                        pool.indirect_dma_start(out, bass.IndirectOffsetOnAxis(mine[:, t:t + 1], 0), acc[:, t, :], None).then_inc(rows_stored, 16)

            for f in range(FT):
                pool.sem_inc(up_lo[f], 1)
            for c in range(2):
                pool.sem_inc(down_lo[c], 1)
            pool.sem_inc(logs, 4)
            pool.sem_inc(own_v_ready, 2)
            pool.memset(minus_half[:], -0.5).then_inc(half_set, 1)
            pool.wait_ge(half_set, 1)
            split_up(0, 0)
            split_up(1, 0)
            split_down(0, 0)
            weave(-1, False, True)
            with pool.Fori(0, B - 1) as b:
                weave(b, True, True)
            weave(B - 1, True, False)
            pool.wait_ge(rows_stored, B * 64)

        @block.scalar
        def _(act):
            def round_up(f, number):
                act.wait_ge(up_in[f], number * 16 + 16)
                act.wait_ge(up_done[f], number + 1)
                act.activation(up_w_hi[:, f, :], up_raw[:, f, :], ACT.Copy).then_inc(up_hi[f], 1)

            def round_down(c, number):
                act.wait_ge(down_in[c], number * 16 + 16)
                act.wait_ge(down_done[c], number * 4 + 5)
                act.activation(down_w_hi[:, c, :], down_raw[:, c, :], ACT.Copy).then_inc(down_hi[c], 1)

            def hidden(N, j, slot):
                for f in range(FT):
                    act.wait_ge(up_done[f], N + 2)
                    hold(act, h_lo_ready, 2 * N + f + 1, held["act"])
                    act.activation(h[:, f, :], h_ps[:, f, :], ACT.Gelu_apprx_tanh, bias=b1[:, ds(j * FT + f, 1)]).then_inc(h_ready, 1)
                for f in range(FT):
                    act.wait_ge(h_ready, 2 * N + f + 3)
                    act.wait_ge(down_done[1], 4 * N + 1)
                    act.activation(h_hi[:, slot, f, :], h[:, f, :], ACT.Copy).then_inc(h_hi_ready, 1)

            def unit_guess(U, s):
                act.wait_ge(den_ready, U + 2)
                act.wait_ge(refined, 2 * U + 4)
                act.activation(guess[:], own[:, s % 2, :], ACT.Ln).then_inc(guessed, 1)
                act.wait_ge(guessed, 2 * U + 1)
                act.activation(guess[:], guess[:], ACT.Exp, scale=-1.0).then_inc(guessed, 1)

            def unit_exps(U, s, column):
                act.wait_ge(logs, 3 * U + 6)
                act.activation(new[:, s % 2, :], new[:, s % 2, :], ACT.Exp).then_inc(exps, 1)
                hold(act, logs, 3 * U + 7, held["act"])
                act.activation(decay[:, s % 2, :], decay[:, s % 2, :], ACT.Exp, bias=w_col[:, ds(column, 1)]).then_inc(exps, 1)
                act.wait_ge(clamped, U + 2)
                act.activation(own[:, s % 2, :], own[:, s % 2, :], ACT.Exp).then_inc(exps, 1)

            def store_y(U, s, pair, block):
                act.wait_ge(y_turned, U + 3)
                act.wait_ge(y_stored[s % 2], pair * 16 + 16)
                act.activation(y_tok[:, s % 2], y_ps[:, s % 2, :].rearrange("p (t c) -> p t c", c=P), ACT.Copy).then_inc(y_evac, 1)
                act.wait_ge(y_evac, U + 3)
                act.dma_start(y_dram[ds(block + s % 2 * HALF, HALF), s // 2 * P:(s // 2 + 1) * P].rearrange("(t p) c -> p t c", p=P),
                              y_tok[:, s % 2]).then_inc(y_stored[s % 2], 16)

            def weave(b, ffn, nxt):
                a = b + 1
                if ffn:
                    for t in range(ST):
                        act.wait_ge(tr_done, b * ST + t + 1)
                        src = (h_ps[:] if t % 2 == 0 else o_ps[:, 0:2, :]).rearrange("p a (k t) -> p (a k) t", t=P)
                        act.activation(xT_hi[:, :, t * P:(t + 1) * P], src, ACT.Copy).then_inc(xt_hi, 1)
                    for f in range(FT):
                        round_up(f, b * STEPS + 1)
                    hidden(b * STEPS, 0, 0)
                with act.Fori(0, LOOPS) as i:
                    for jj in range(LOOP_STEPS):
                        j = i * LOOP_STEPS + jj
                        n = b * STEPS + j
                        if ffn:
                            round_down(1, n)
                        for half in range(2):
                            if ffn and half == 1:
                                round_up(0, n + 2)
                                round_down(0, n + 1)
                                round_up(1, n + 2)
                                hidden(n + 1, j + 1, (jj + 1) % 2)
                            if nxt:
                                for s in range(LOOP_UNITS + 1):
                                    U = a * UNITS + i * LOOP_UNITS + s
                                    pair = a * (UNITS // 2) + i * (LOOP_UNITS // 2) + s // 2
                                    if half_of(5 * s + 3) == 2 * jj + half:
                                        if s >= 1:
                                            unit_guess(U - 1, s - 1)
                                        if s < LOOP_UNITS:
                                            unit_exps(U, s, i * (KT // 2) + s // 2)
                                    if s < LOOP_UNITS and turn_half(s) == 2 * jj + half:
                                        store_y(U, s, pair, (a * LOOPS + i) * T)
                    if nxt:
                        for s in range(LOOP_UNITS):
                            if turn_half(s) >= 2 * LOOP_STEPS:
                                store_y(a * UNITS + i * LOOP_UNITS + s, s, a * (UNITS // 2) + i * (LOOP_UNITS // 2) + s // 2,
                                        (a * LOOPS + i) * T)
                if nxt and not (isinstance(a, int) and a == 0):
                    hold(act, x2_in, a * 64, held["act"])
                for jj in range(REST):
                    j = STEPS - REST + jj
                    n = b * STEPS + j
                    if ffn:
                        round_down(1, n)
                    for half in range(2):
                        if ffn and half == 1:
                            if j < STEPS - 1 and not (j == STEPS - 2 and not nxt):
                                round_up(0, n + 2)
                            if nxt or j < STEPS - 1:
                                round_down(0, n + 1)
                            if j < STEPS - 1 and not (j == STEPS - 2 and not nxt):
                                round_up(1, n + 2)
                            if j < STEPS - 1:
                                hidden(n + 1, j + 1, (j + 1) % 2)
                        if nxt:
                            for t in range(TT):
                                if half_of(head_place(t)) == 2 * jj + half:
                                    act.wait_ge(row_ready, a * TT + t + 1)
                                    act.dma_start(out[ds(a * T, T), :].rearrange("(p t) c -> p t c", t=TT)[:, t, :], row_x[t % 4]).then_inc(row_stored[t % 4], 16)
                                    act.dma_start(x2_dram.rearrange("(p t) c -> p t c", t=TT)[:, t, :], row_x[t % 4]).then_inc(row_stored[t % 4], 16)

            for s in range(2):
                act.sem_inc(y_stored[s], 16)
            act.sem_inc(y_evac, 2)
            act.sem_inc(h_ready, 2)
            act.wait_ge(const_in, 144)
            round_up(0, 0)
            round_up(1, 0)
            round_down(0, 0)
            weave(-1, False, True)
            with act.Fori(0, B - 1) as b:
                weave(b, True, True)
            weave(B - 1, True, False)

        @block.vector
        def _(dve):
            def unit_top(U, s, loads, number, column):
                if s % 2 == 0:
                    dve.wait_ge(clamped, U + 1)
                    dve.wait_ge(top_ready, U + 1)
                    dve.tensor_copy(w_now[:, 0:1], w_col[:, ds(column, 1)]).then_inc(column_ready, 1)
                    dve.tensor_copy(w_now[:, 1:2], u_col[:, ds(column, 1)]).then_inc(column_ready, 1)
                    dve.wait_ge(column_ready, number * 2 + 2)
                dve.wait_ge(k_in[s % 2], loads)
                dve.wait_ge(logs, 3 * U + 4)
                lo = s % 2 * HALF
                dve.wait_ge(top_ready, U + 1)
                dve.tensor_tensor_scan(top[:, lo + 1:lo + HALF + 1], w_now[:, 0:1].to_broadcast([P, HALF]), k[:, s % 2, :],
                                       top[:, HALF:HALF + 1] if s % 2 else NO_PAST, ALU.add, ALU.max).then_inc(top_ready, 1)

            def unit_clamp(U, s):
                dve.wait_ge(logs, 3 * U + 5)
                dve.tensor_scalar(own[:, s % 2, :], own[:, s % 2, :], w_now[:, 1:2], R_CLAMP, ALU.add, ALU.min).then_inc(clamped, 1)

            def unit_q(U, s, loads):
                lo = s % 2 * HALF
                dve.wait_ge(exps, 3 * U + 2)
                dve.wait_ge(v_in[s % 2], loads)
                dve.wait_ge(state, 2 * U + 3)
                dve.tensor_tensor(new_v[:], new[:, s % 2, :], v[:, s % 2, :], ALU.mult).then_inc(new_v_ready, 1)
                dve.wait_ge(den_ready, U + 1)
                dve.tensor_tensor_scan(q[:, lo + 1:lo + HALF + 1], decay[:, s % 2, :], new[:, s % 2, :],
                                       q[:, HALF:HALF + 1] if s % 2 else 0.0, ALU.mult, ALU.add).then_inc(state, 1)

            def unit_p(U, s):
                lo = s % 2 * HALF
                dve.wait_ge(new_v_ready, U + 3)
                dve.wait_ge(num_ready, U + 1)
                dve.tensor_tensor_scan(p[:, lo + 1:lo + HALF + 1], decay[:, s % 2, :], new_v[:],
                                       p[:, HALF:HALF + 1] if s % 2 else 0.0, ALU.mult, ALU.add).then_inc(state, 1)
                dve.wait_ge(own_v_ready, U + 3)
                dve.wait_ge(state, 2 * U + 4)
                dve.tensor_tensor(own[:, s % 2, :], own[:, s % 2, :], q[:, lo:lo + HALF], ALU.add).then_inc(den_ready, 1)

            def unit_num(U, s):
                lo = s % 2 * HALF
                dve.wait_ge(state, 2 * U + 5)
                dve.tensor_tensor(own_v[:, s % 2, :], own_v[:, s % 2, :], p[:, lo:lo + HALF], ALU.add).then_inc(num_ready, 1)

            def unit_y(U, s):
                dve.wait_ge(guessed, 2 * U + 2)
                dve.wait_ge(y_ready, U + 2)
                dve.tensor_tensor(better[:], own[:, s % 2, :], guess[:], ALU.mult).then_inc(refined, 1)
                dve.wait_ge(refined, 2 * U + 5)
                dve.scalar_tensor_tensor(better[:], better[:], 2.0, guess[:], ALU.subtract, ALU.mult).then_inc(refined, 1)
                dve.wait_ge(refined, 2 * U + 6)
                dve.wait_ge(num_ready, U + 2)
                dve.wait_ge(y_turned, U + 1)
                dve.scalar_tensor_tensor(y[:, s % 2, :], own_v[:, s % 2, :], -1.0, better[:], ALU.mult, ALU.mult).then_inc(y_ready, 1)

            def add(n, place):
                c, t = place // 4, place % 4
                dve.wait_ge(down_done[c], 4 * n + t + 6)
                dve.wait_ge(added, 8 * n + place + 1)
                dve.tensor_tensor(acc[:, t, c * HALF:(c + 1) * HALF], o_ps[:, t, :], acc[:, t, c * HALF:(c + 1) * HALF], ALU.add).then_inc(added, 1)

            def split_hidden(N, slot):
                for f in range(FT):
                    dve.wait_ge(h_hi_ready, 2 * N + f + 1)
                    dve.tensor_tensor(h_lo[:, slot, f, :], h[:, f, :], h_hi[:, slot, f, :].bitcast(F32), ALU.subtract).then_inc(h_lo_ready, 1)

            def row_head(a, t):
                s = t % 2
                first = (a * TT + t) * 3
                dve.wait_ge(row_x_in[t % 4], a * 32 + t // 4 * 16 + 16)
                dve.wait_ge(row_y_in[s], a * 64 + t // 2 * 16 + 16)
                dve.tensor_tensor(row_x[t % 4], row_x[t % 4], row_y[s], ALU.add).then_inc(row_ready, 1)
                if not (isinstance(a, int) and a == 0 and t < 2):
                    hold(dve, s_norm, a * TT + t - 1, held["dve"])
                hold(dve, row_ready, a * TT + t + 1, held["dve"])
                for g in range(2):
                    dve.bn_stats(s_stats[:, s, g, :], row_x[t % 4][:, g * HALF:(g + 1) * HALF]).then_inc(s_step, 1)
                hold(dve, s_step, first + 2, held["dve"])
                dve.bn_aggr(s_mv[:, s, :], s_stats[:, s]).then_inc(s_step, 1)
                dve.wait_ge(s_step, first + 3)
                dve.tensor_scalar(s_var[:, s:s + 1], s_mv[:, s, 1:2], LN_EPS, None, ALU.add).then_inc(s_var_ready, 1)

            def row_tail(a, t):
                s = t % 2
                dve.wait_ge(s_rstd_ready, a * TT + t + 1)
                dve.tensor_scalar(row_y[s], row_x[t % 4], s_mv[:, s, 0:1], s_rstd[:, s:s + 1], ALU.subtract, ALU.mult).then_inc(s_norm, 1)
                dve.wait_ge(s_norm, a * TT + t + 1)
                if not (isinstance(a, int) and a == 0 and t == 0):
                    dve.wait_ge(s_product, a * TT + t)
                dve.tensor_tensor_reduce(scrap, row_y[s], w_r[:], 1.0, 0.0, ALU.mult, ALU.add,
                                         product[:, t:t + 1]).then_inc(s_product, 1)

            def row_rank(a, t):
                if t == 0:
                    dve.wait_ge(scores_in, a * 16 + 16)
                else:
                    dve.wait_ge(ranked, a * TT + t)
                dve.scalar_tensor_tensor(scrap, all_scores, score[:, t:t + 1], tie[:, TT - 1 - t:TT - 1 - t + T],
                                         ALU.subtract, ALU.is_gt, accum_out=rank[:, t:t + 1]).then_inc(ranked, 1)

            def choose(a, place):
                for t in range(TT):
                    if head_place(t) + 2 == place:
                        row_tail(a, t)
                    if head_place(t) == place:
                        row_head(a, t)
                if place == 19:
                    dve.wait_ge(s_product, a * TT + TT)
                    dve.tensor_scalar(score[:], product[:], b_r[:, 0:1], None, ALU.add).then_inc(score_ready, 1)
                if 22 <= place < 26:
                    if place == 22:
                        dve.wait_ge(score_ready, a + 1)
                    row_rank(a, (place - 22) * 2)
                    row_rank(a, (place - 22) * 2 + 1)
                if place == 25:
                    dve.wait_ge(ranked, a * TT + TT)
                    dve.tensor_copy(rank_i[:], rank[:]).then_inc(order_ready, 1)

            def norm_statistics(a, place):
                if place == REST * 8 - 1:
                    if not (isinstance(a, int) and a == 0):
                        hold(dve, xn_ready, a * ST, held["dve"])
                    hold(dve, x2_in, a * 64 + 64, held["dve"])
                    for t in range(ST):
                        for g in range(2):
                            dve.bn_stats(stats[:, t, g, :], x2[:, t, g * HALF:(g + 1) * HALF]).then_inc(ln_step, 1)
                    for t in range(ST):
                        hold(dve, ln_step, a * 12 + 8, held["dve"])
                        dve.bn_aggr(mv[:, t, :], stats[:, t]).then_inc(ln_step, 1)
                    for t in range(ST):
                        dve.wait_ge(ln_step, a * 12 + 12)
                        dve.tensor_scalar(var_eps[:, t:t + 1], mv[:, t, 1:2], LN_EPS, None, ALU.add).then_inc(var_ready, 1)

            def weave(b, ffn, nxt):
                a = b + 1
                if ffn:
                    for t in range(ST + 1):
                        if t < ST:
                            dve.wait_ge(rstd_ready, b + 1)
                            if t >= 1:
                                dve.wait_ge(tr_done, b * ST + t)
                            dve.tensor_scalar(xn[:], x2[:, t, :], mv[:, t, 0:1], rstd[:, t:t + 1], ALU.subtract,
                                              ALU.mult).then_inc(xn_ready, 1)
                        if t >= 1:
                            src = (h_ps[:] if (t - 1) % 2 == 0 else o_ps[:, 0:2, :]).rearrange("p a (k t) -> p (a k) t", t=P)
                            dve.wait_ge(xt_hi, b * ST + t)
                            dve.tensor_tensor(xT_lo[:, :, (t - 1) * P:t * P], src, xT_hi[:, :, (t - 1) * P:t * P].bitcast(F32),
                                              ALU.subtract).then_inc(xt_lo, 1)
                    dve.wait_ge(rows_left, b + 1)
                    dve.wait_ge(first_row_set, b + 1)
                    dve.tensor_scalar(mine[:], chosen[:], first_row[:, 0:1], None, ALU.add).then_inc(mine_set, 1)
                    dve.wait_ge(mine_set, b + 1)
                    dve.tensor_scalar(first_row[:], first_row[:], float(T), None, ALU.add).then_inc(first_row_set, 1)
                    for t in range(ST):
                        dve.wait_ge(added, b * STEPS * 8 + 4)
                        dve.tensor_tensor(acc[:, t, :], x2[:, t, :], b2[:], ALU.add).then_inc(acc_set, 1)
                    split_hidden(b * STEPS, 0)
                    dve.wait_ge(acc_set, b * ST + ST)
                    dve.sem_inc(held["dve"], 1)
                with dve.Fori(0, LOOPS) as i:
                    for place in range(LOOP_STEPS * 8):
                        jj = place // 8
                        n = b * STEPS + i * LOOP_STEPS + jj
                        if ffn:
                            add(n, place % 8)
                        if nxt:
                            s, r = place // 5, place % 5
                            U = a * UNITS + i * LOOP_UNITS + s
                            pair = a * (UNITS // 2) + i * (LOOP_UNITS // 2)
                            if r == 0 and s < LOOP_UNITS:
                                unit_top(U, s, (pair + s // 2) * 16 + 16, a * KT + i * (KT // 2) + s // 2, i * (KT // 2) + s // 2)
                            if r == 0 and s >= 2:
                                unit_y(U - 2, s - 2)
                            if r == 1 and 1 <= s <= LOOP_UNITS:
                                unit_q(U - 1, s - 1, (pair + (s - 1) // 2) * 16 + 16)
                            if r == 2 and 1 <= s <= LOOP_UNITS:
                                unit_p(U - 1, s - 1)
                            if r == 3 and s < LOOP_UNITS:
                                unit_clamp(U, s)
                            if r == 3 and 1 <= s <= LOOP_UNITS:
                                unit_num(U - 1, s - 1)
                        if ffn and place % 8 == 5:
                            split_hidden(n + 1, (jj + 1) % 2)
                for place in range(REST * 8):
                    j = STEPS - REST + place // 8
                    n = b * STEPS + j
                    if ffn:
                        add(n, place % 8)
                    if nxt:
                        choose(a, place)
                        norm_statistics(a, place)
                    if ffn and place % 8 == 5 and j < STEPS - 1:
                        split_hidden(n + 1, (j + 1) % 2)

            for c, credit in ((new_v_ready, 2), (state, 3), (den_ready, 1), (num_ready, 1), (refined, 4), (y_ready, 2),
                              (h_lo_ready, 2), (added, 4), (clamped, 1), (top_ready, 1)):
                dve.sem_inc(c, credit)
            dve.memset(top[:, 0:1], NO_PAST).then_inc(start_set, 1)
            dve.memset(p[:, 0:1], 0.0).then_inc(start_set, 1)
            dve.memset(q[:, 0:1], 0.0).then_inc(start_set, 1)
            dve.wait_ge(const_in, 144)
            dve.tensor_copy(tok_i[:], tok[:]).then_inc(start_set, 1)
            dve.memset(first_row[:], 0.0).then_inc(first_row_set, 1)
            dve.wait_ge(start_set, 4)
            dve.sem_inc(held["dve"], 1)
            weave(-1, False, True)
            with dve.Fori(0, B - 1) as b:
                weave(b, True, True)
            weave(B - 1, True, False)

        @block.tensor
        def _(pe):
            def up(f, N):
                pe.wait_ge(up_lo[f], N + 2)
                pe.wait_ge(h_ready, 2 * N + f + 1)
                for kk in range(KT):
                    mm = product3(pe, h_ps[:, f, :], up_w_hi[:, f, kk * P:(kk + 1) * P], up_w_lo[:, f, kk * P:(kk + 1) * P],
                                  xT_hi[:, kk, :], xT_lo[:, kk, :], kk == 0, kk == KT - 1)
                mm.then_inc(up_done[f], 1)

            def down(c, n, slot):
                pe.wait_ge(down_lo[c], n + 2)
                pe.wait_ge(h_lo_ready, 2 * n + 4)
                for t in range(ST):
                    pe.wait_ge(added, 8 * n + 4 * c + t + 1)
                    for f in range(FT):
                        mm = product3(pe, o_ps[:, t, :], h_hi[:, slot, f, t * P:(t + 1) * P], h_lo[:, slot, f, t * P:(t + 1) * P],
                                      down_w_hi[:, c, f * HALF:(f + 1) * HALF], down_w_lo[:, c, f * HALF:(f + 1) * HALF],
                                      f == 0, f == FT - 1)
                    mm.then_inc(down_done[c], 1)

            def turn(U, s):
                pe.wait_ge(y_ready, U + 3)
                pe.wait_ge(y_evac, U + 1)
                for t in range(HALF // P):
                    mm = pe.transpose(y_ps[:, s % 2, t * P:(t + 1) * P], y[:, s % 2, t * P:(t + 1) * P], ident[:])
                mm.then_inc(y_turned, 1)

            def weave(b, ffn, nxt):
                a = b + 1
                if ffn:
                    for t in range(ST):
                        pe.wait_ge(xn_ready, b * ST + t + 1)
                        if t == 0:
                            pe.wait_ge(added, b * STEPS * 8 + 4)
                        if t >= 2:
                            pe.wait_ge(xt_lo, b * ST + t - 1)
                        dst = h_ps[:] if t % 2 == 0 else o_ps[:, 0:2, :]
                        for kk in range(KT):
                            mm = pe.transpose(dst[:, kk // 4, kk % 4 * P:kk % 4 * P + P], xn[:, kk * P:(kk + 1) * P], ident[:])
                        mm.then_inc(tr_done, 1)
                    pe.wait_ge(xt_lo, b * ST + ST)
                    up(0, b * STEPS)
                    up(1, b * STEPS)
                with pe.Fori(0, LOOPS) as i:
                    for jj in range(LOOP_STEPS):
                        n = b * STEPS + i * LOOP_STEPS + jj
                        for half in range(2):
                            if ffn:
                                up(half, n + 1)
                                down(half, n, jj % 2)
                            if nxt:
                                for s in range(LOOP_UNITS):
                                    if turn_half(s) == 2 * jj + half:
                                        turn(a * UNITS + i * LOOP_UNITS + s, s)
                    if nxt:
                        for s in range(LOOP_UNITS):
                            if turn_half(s) >= 2 * LOOP_STEPS:
                                turn(a * UNITS + i * LOOP_UNITS + s, s)
                if ffn:
                    for jj in range(REST):
                        j = STEPS - REST + jj
                        n = b * STEPS + j
                        for half in range(2):
                            if j < STEPS - 1:
                                up(half, n + 1)
                            down(half, n, j % 2)

            for f in range(FT):
                pe.sem_inc(up_done[f], 1)
                pe.sem_inc(down_done[f], 5)
            pe.sem_inc(y_turned, 2)
            pe.wait_ge(const_in, 144)
            pe.sem_inc(held["pe"], 1)
            weave(-1, False, True)
            with pe.Fori(0, B - 1) as b:
                weave(b, True, True)
            weave(B - 1, True, False)


def build(nc, x, ctxT, w_kvq, w_p, b_p, w_decay, u_bonus, w_r, b_r, w1, b1, w2, b2, head_mask, identity, tie, token, out):
    x1_dram = nc.dram_tensor("x1", [B * T, C], F32).ap()
    kT_dram = nc.dram_tensor("kT", [B * C, T], F32).ap()
    y_dram = nc.dram_tensor("y", [B * 2 * T, C // 2], F32).ap()
    score_dram = nc.dram_tensor("score", [B * T], F32).ap()
    x2_dram = nc.dram_tensor("x2", [T, C], F32).ap()
    order_dram = nc.dram_tensor("order", [T, 1], I32).ap()
    attention_phase(nc, x, w_kvq, w_p, b_p, head_mask, identity, x1_dram, kT_dram)
    wkv_ffn_phase(nc, kT_dram, ctxT, x1_dram, w_decay, u_bonus, w_r, b_r, w1, b1, w2, b2, tie, token, identity,
                  y_dram, x2_dram, score_dram, order_dram, out)


def kernel(x, ctx_2048, L0_attn_w_qkv, L0_attn_w_proj, L0_attn_b_proj, L0_xattn_w, L0_xattn_u, L0_ffn_w_r, L0_ffn_b_r,
           L0_ffn_w1, L0_ffn_b1, L0_ffn_w2, L0_ffn_b2):
    import numpy as np
    import concourse.bacc as bacc
    from concourse.bass_utils import run_bass_kernel_spmd

    def tiled(w, cols):
        k, n = w.shape[0] // P, w.shape[1] // cols
        return w.reshape(k, P, n, cols).transpose(2, 1, 0, 3).reshape(n * P, k * cols)

    def columns(v):
        return v.reshape(-1, P).T

    w_q, w_k, w_v = (np.asarray(L0_attn_w_qkv)[i * C:(i + 1) * C].T for i in range(3))
    w_kv = np.stack([w_k.reshape(C, KT, P), w_v.reshape(C, KT, P)], axis=2).reshape(C, 2 * C)
    part, col = np.arange(P)[:, None], np.arange(T)[None, :]
    token = TT * part + np.arange(TT)[None, :]
    arrays = {
        "x": np.asarray(x).reshape(B * T, C),
        "ctxT": np.asarray(ctx_2048).transpose(0, 2, 1).reshape(B * C, T),
        "w_kvq": np.concatenate([tiled(w_kv, 256), tiled(w_q, 256)]),
        "w_p": tiled(np.asarray(L0_attn_w_proj).T, 256),
        "b_p": np.asarray(L0_attn_b_proj),
        "w_decay": columns(np.asarray(L0_xattn_w)),
        "u_bonus": columns(np.asarray(L0_xattn_u)),
        "w_r": np.asarray(L0_ffn_w_r),
        "b_r": np.asarray(L0_ffn_b_r).reshape(1),
        "w1": tiled(np.asarray(L0_ffn_w1), P),
        "b1": columns(np.asarray(L0_ffn_b1)),
        "w2": np.asarray(L0_ffn_w2),
        "b2": np.asarray(L0_ffn_b2),
        "head_mask": (part // HEAD == col[:, :P] // HEAD).astype(np.float32),
        "identity": np.eye(P, dtype=np.float32),
        "tie": np.where(np.arange(T + TT)[None, :] - (TT - 1) < TT * part, JUST_BELOW_0, 0.0).astype(np.float32),
        "token": token.astype(np.float32),
    }
    nc = bacc.Bacc("TRN2", target_bir_lowering=False, num_devices=1)
    args = []
    for name, a in arrays.items():
        arrays[name] = a = np.ascontiguousarray(a)
        args.append(nc.dram_tensor(name, a.shape, mybir.dt.from_np(a.dtype), kind="ExternalInput").ap())
    args.append(nc.dram_tensor("out", (B * T, C), F32, kind="ExternalOutput").ap())
    build(nc, *args)
    r = run_bass_kernel_spmd(nc, [arrays], core_ids=[0])
    return r.results[0]["out"].reshape(B, T, C)
```
